# Optimizing a Trainium2 kernel written in Bass

```python
import numpy as np
import jax
import jax.numpy as jnp

def _softmax(x, axis=-1):
    return jax.nn.softmax(x, axis=axis)

def _gelu(x):
    return jax.nn.gelu(x, approximate=True)

def _silu(x):
    return jax.nn.silu(x)

def _sigmoid(x):
    return jax.nn.sigmoid(x)

def _layernorm(x, axis=-1, eps=1e-05):
    m = jnp.mean(x, axis=axis, keepdims=True)
    v = jnp.var(x, axis=axis, keepdims=True)
    return (x - m) / jnp.sqrt(v + eps)

def _scatter_add(tgt, idx, src, axis=0):
    return tgt.at[idx].add(src)

def _segment_sum(src, seg, n):
    return jax.ops.segment_sum(src, seg, n)
kernel_name = 'mk_seq_postln_d1_jaxref_r2_29f903'

def setup_inputs(seed: int=0):
    np.random.seed(seed)
    _w = jnp.asarray

    def _L0_attn_setup():
        import jax, jax.numpy as jnp
        import numpy as np
        B, S, D = (8, 2048, 512)
        H, DK, DV, L = (8, 64, 64, 128)
        key = jax.random.key(seed)
        ks = jax.random.split(key, 6)
        x = jax.random.normal(ks[0], (B, S, D), dtype=jnp.float32)
        sd = 1.0 / np.sqrt(D)
        Wq = jax.random.normal(ks[1], (D, H * DK), dtype=jnp.float32) * sd
        Wk = jax.random.normal(ks[2], (D, H * DK), dtype=jnp.float32) * sd
        Wv = jax.random.normal(ks[3], (D, H * DV), dtype=jnp.float32) * sd
        betas = jax.random.normal(ks[4], (1, H, 1, DV), dtype=jnp.float32)
        Wo = jax.random.normal(ks[5], (H * DV, D), dtype=jnp.float32) * (1.0 / np.sqrt(H * DV))
        return {'x': x, 'Wq': Wq, 'Wk': Wk, 'Wv': Wv, 'betas': betas, 'Wo': Wo}
    _L0_attn_in = _L0_attn_setup()

    def _L0_ffn_setup():
        import jax, jax.numpy as jnp
        import numpy as np
        EPS = 1e-05

        def _quantize(W):
            gamma = jnp.mean(jnp.abs(W))
            return jnp.clip(jnp.round(W / (gamma + EPS)), -1.0, 1.0)
        key = jax.random.key(seed)
        k_x, k_w1, k_b1, k_w2, k_b2 = jax.random.split(key, 5)
        n_embd = 512
        d_ff = 4 * n_embd
        B, S = (4, 2048)
        bound1 = 1.0 / np.sqrt(n_embd)
        bound2 = 1.0 / np.sqrt(d_ff)
        x = jax.random.normal(k_x, (B, S, n_embd), dtype=jnp.float32)
        W1 = jax.random.uniform(k_w1, (d_ff, n_embd), jnp.float32, -bound1, bound1)
        b1 = jax.random.uniform(k_b1, (d_ff,), jnp.float32, -bound1, bound1)
        W2 = jax.random.uniform(k_w2, (n_embd, d_ff), jnp.float32, -bound2, bound2)
        b2 = jax.random.uniform(k_b2, (n_embd,), jnp.float32, -bound2, bound2)
        return {'x': x, 'W1': W1, 'b1': b1, 'W2': W2, 'b2': b2}
    _L0_ffn_in = _L0_ffn_setup()
    _d = {'L0_attn_x': _L0_attn_in['x'], 'L0_attn_Wq': _L0_attn_in['Wq'], 'L0_attn_Wk': _L0_attn_in['Wk'], 'L0_attn_Wv': _L0_attn_in['Wv'], 'L0_attn_betas': _L0_attn_in['betas'], 'L0_attn_Wo': _L0_attn_in['Wo'], 'L0_ffn_W1': _L0_ffn_in['W1'], 'L0_ffn_b1': _L0_ffn_in['b1'], 'L0_ffn_W2': _L0_ffn_in['W2'], 'L0_ffn_b2': _L0_ffn_in['b2']}
    _x0 = _d['L0_attn_x']
    _d['L0_attn_x'] = jax.random.normal(jax.random.fold_in(jax.random.key(seed), 1), (8, 1024, 512), dtype=_x0.dtype)
    del _x0
    return _d

def reference(L0_attn_x, L0_attn_Wq, L0_attn_Wk, L0_attn_Wv, L0_attn_betas, L0_attn_Wo, L0_ffn_W1, L0_ffn_b1, L0_ffn_W2, L0_ffn_b2):

    def _L0_attn_ref(x, Wq, Wk, Wv, betas, Wo):
        import jax, jax.numpy as jnp
        import numpy as np
        B, S, D = (8, 2048, 512)
        H, DK, DV, L = (8, 64, 64, 128)
        b, s, d = x.shape
        n_seq = s // L
        xs = x.reshape(b, n_seq, L, d)

        def proj(W, dh):
            p = xs @ W
            return p.reshape(b, n_seq, L, H, dh).transpose(1, 0, 3, 2, 4)
        q = proj(Wq, DK)
        k = proj(Wk, DK)
        v = proj(Wv, DV)
        scale = 1.0 / np.sqrt(DK)
        gate = jax.nn.sigmoid(betas)
        mem0 = jnp.zeros((b, H, DK, DV), dtype=x.dtype)
        z0 = jnp.ones((b, H, DK, 1), dtype=x.dtype) / DK

        def step(carry, inp):
            mem, z = carry
            q_s, k_s, v_s = inp
            sq = jax.nn.elu(q_s) + 1.0
            att_mem = sq @ mem / (sq @ z)
            sk = jax.nn.elu(k_s) + 1.0
            mem = mem + jnp.einsum('bhlk,bhlv->bhkv', sk, v_s)
            z = z + sk.sum(axis=-2, keepdims=True).transpose(0, 1, 3, 2)
            att_dot = jax.nn.softmax(jnp.einsum('bhik,bhjk->bhij', q_s, k_s) * scale, axis=-1)
            att = att_dot @ v_s
            att = gate * att_mem + (1.0 - gate) * att
            return ((mem, z), att)
        _, outs = jax.lax.scan(step, (mem0, z0), (q, k, v))
        out = outs.transpose(1, 0, 3, 2, 4).reshape(b, s, H * DV)
        return out @ Wo

    def _L0_ffn_ref(x, W1, b1, W2, b2):
        import jax, jax.numpy as jnp
        import numpy as np
        EPS = 1e-05

        def _quantize(W):
            gamma = jnp.mean(jnp.abs(W))
            return jnp.clip(jnp.round(W / (gamma + EPS)), -1.0, 1.0)
        Wq1 = _quantize(W1)
        Wq2 = _quantize(W2)
        h = jax.nn.relu(jnp.einsum('bsd,fd->bsf', x, Wq1) + b1)
        out = jnp.einsum('bsf,df->bsd', h, Wq2) + b2
        return out
    x = L0_attn_x
    x = _layernorm(x + _L0_attn_ref(x, L0_attn_Wq, L0_attn_Wk, L0_attn_Wv, L0_attn_betas, L0_attn_Wo), axis=-1)
    x = _layernorm(x + _L0_ffn_ref(x, L0_ffn_W1, L0_ffn_b1, L0_ffn_W2, L0_ffn_b2), axis=-1)
    return x

_drawn_inputs = setup_inputs


def setup_inputs(seed=0):
    import zlib

    import numpy as np

    out = dict(_drawn_inputs(seed))
    spreads = {}
    factors = {'L0_ffn_b1': 43.484, 'L0_ffn_b2': 64.0}
    for name, (base, spread) in spreads.items():
        noise = np.random.default_rng([zlib.crc32(name.encode()), seed]).standard_normal(out[name].shape)
        drawn = base * np.exp(spread * noise) if base else spread * noise
        out[name] = jnp.asarray(drawn.astype(out[name].dtype))
    for name, factor in factors.items():
        out[name] = (out[name] * factor).astype(out[name].dtype)
    return out
```

```python
from contextlib import ExitStack

import concourse.bass as bass
import concourse.mybir as mybir

ALU = mybir.AluOpType
ACT = mybir.ActivationFunctionType
F32 = mybir.dt.float32
F16 = mybir.dt.float16
U32 = mybir.dt.uint32
AX_X = mybir.AxisListType.X
AX_XY = mybir.AxisListType.XY
RMAX = bass.bass_isa.ReduceOp.max
RADD = bass.bass_isa.ReduceOp.add

P = 128
RING = 7
EXPONENT = 0x7F800000
EPS = 1e-5


class Signal:

    def __init__(self, sem):
        self.sem = sem
        self.count = 0


class Queue:

    def __init__(self):
        self.items = []
        self.waited = {}

    def add(self, emit, after=(), signal=None, by=1):
        waits = []
        for token in after:
            if token is None:
                continue
            sem, value = token
            if self.waited.get(id(sem), 0) < value:
                self.waited[id(sem)] = value
                waits.append(token)
        if signal is not None:
            signal.count += by
        self.items.append((waits, emit, signal.sem if signal else None, by))
        return (signal.sem, signal.count) if signal else None

    def replay(self, eng):
        for waits, emit, sem, by in self.items:
            for s, value in waits:
                eng.wait_ge(s, value)
            ins = emit(eng) if emit else None
            if sem is not None:
                ins.then_inc(sem, by)


def build_program(nc, x, Wq, Wk, Wv, betas, Wo, W1, b1, W2, b2, out):
    B, S, D = x.shape
    H, DV = betas.shape[1], betas.shape[3]
    DK = Wq.shape[1] // H
    F = W1.shape[0]
    KT = D // P
    FT = F // P
    NPAIR = H * DK // P
    NSEG = S // P
    TG = 2
    GT = TG * P
    LIVE = 2
    NG = B // TG * NSEG
    DV1 = DV + 1
    assert DK == DV == 64 and D == 512 and H == 8 and B % (TG * LIVE) == 0 and S % P == 0

    ctx = ExitStack()
    with ctx:
        def sb(name, shape, dt=F32):
            return ctx.enter_context(nc.sbuf_tensor(name, shape, dt))

        def signal(name):
            return Signal(ctx.enter_context(nc.semaphore(name)))

        banks = [ctx.enter_context(nc.psum_tensor(f"bank{i}", [P, 512], F32)) for i in range(8)]

        w_hi = {n: sb(f"w{n}_hi", [P, KT, D], F16) for n in "kqvo"}
        w_lo = {n: sb(f"w{n}_lo", [P, KT, D], F16) for n in "kqvo"}
        w1t = sb("w1t", [P, KT, F], F16)
        w2t = sb("w2t", [P, FT, D], F16)
        arena = sb("arena", [P, 4, 2048], F32)
        wquant = sb("wquant", [P, 2, 512], F16)
        wbelow = sb("wbelow", [P, 2, 512], F16)
        ident32 = sb("ident32", [P, P])
        ident16 = sb("ident16", [P, P], F16)
        gate_in = sb("gate_in", [P, D])
        gate_out = sb("gate_out", [P, D])
        b2_all = sb("b2_all", [P, D])
        b1_col = sb("b1_col", [P, FT])
        b1_rows = sb("b1_rows", [FT, P])
        b1_scaled = sb("b1_scaled", [P, FT])
        minus_half = sb("minus_half", [P, 1])
        ws = sb("wscalars", [P, 40])
        gs = sb("gscalars", [P, NG, 16])

        NX = 4
        rows = sb("rows", [P, NX, TG, D])
        xt_hi = sb("xt_hi", [P, KT, GT], F16)
        xt_lo = sb("xt_lo", [P, KT, GT], F16)
        q_hi = sb("q_hi", [P, NPAIR, GT], F16)
        q_lo = sb("q_lo", [P, NPAIR, GT], F16)
        kz_hi = sb("kz_hi", [P, NPAIR, 2, GT], F16)
        kz_lo = sb("kz_lo", [P, NPAIR, 2, GT], F16)
        sq_t = sb("sq_t", [P, NPAIR, GT])
        sk_t = sb("sk_t", [P, NPAIR, GT])
        exp_tmp = sb("exp_tmp", [P, 512])
        relu_tmp = sb("relu_tmp", [P, 512])
        v_hi = sb("v_hi", [P, TG, D], F16)
        v_lo = sb("v_lo", [P, TG, D], F16)
        v1 = sb("v1", [P, TG, H, DV1])
        sk = sb("sk", [P, TG, H * DK])
        prob = sb("prob", [P, TG, H, P])
        pt_hi = sb("pt_hi", [P, TG, H, P], F16)
        pt_lo = sb("pt_lo", [P, TG, H, P], F16)
        att_mem = sb("att_mem", [P, TG, H, DV])
        att_dot = sb("att_dot", [P, TG, H, DV])
        at_hi = sb("at_hi", [P, TG, KT, P], F16)
        at_lo = sb("at_lo", [P, TG, KT, P], F16)
        mem = sb("mem", [P, LIVE * TG, NPAIR, 2 * DV1])
        row_max = sb("row_max", [P, TG, H])
        exp_bias = sb("exp_bias", [P, TG, H])
        row_sum = sb("row_sum", [P, TG, H])
        inv_sum = sb("inv_sum", [P, TG, H])
        dot_scale = sb("dot_scale", [P, TG, H])
        inv_den = sb("inv_den", [P, TG, H])
        amax = sb("amax", [P, 2])
        stats = sb("stats", [P, 2, TG, 6])
        mean_var = sb("mean_var", [P, 2, TG, 2])
        var_eps = sb("var_eps", [P, 2, TG])
        rstd = sb("rstd", [P, 2, TG])

        flat = arena[:].rearrange("p a b -> p (a b)")
        h_hi = flat[:, 0:2048].bitcast(F16).rearrange("p (f t) -> p f t", f=FT)
        h_lo = flat[:, 2048:4096].bitcast(F16).rearrange("p (f t) -> p f t", f=FT)
        yt_hi = flat[:, 4096:5120].bitcast(F16).rearrange("p (b k t) -> p b k t", b=2, k=KT)
        yt_lo = flat[:, 5120:6144].bitcast(F16).rearrange("p (b k t) -> p b k t", b=2, k=KT)
        NH32 = 3
        h32 = flat[:, 6144:6144 + NH32 * 512].rearrange("p (b t) -> p b t", b=NH32)

        names = ("consts gp_work bload "
                 "wmax wsum scal wsplit_hi wsplit_lo quant wturn wput amax_all "
                 "xturn xt_hi xt_lo kproj qproj vproj kq_hi kq_lo kq_exp kq_sk v_hi v_lo v1 "
                 "score smax pexp pturn pt_hi pt_lo pv num skturn sk upd mem den mix_dve mix_pool "
                 "aturn at_hi at_lo wo resid stat pow_in rstd norm yturn yt_hi yt_lo yb "
                 "ffn1 relu h_hi h_lo ffn2 chain actmisc")
        sig = {n: signal("s_" + n) for n in names.split()}

        s_wload = [signal(f"s_wload{i}") for i in range(4)]
        s_xload = [signal(f"s_xload{i}") for i in range(NX)]
        s_xout = [[signal(f"s_xout{i}_{t}") for t in range(TG)] for i in range(NX)]

        pe, act, dve, pool, sp = (Queue() for _ in range(5))
        done = {}

        def after(*keys):
            return [done.get(k) for k in keys]

        bank_free = [[] for _ in range(8)]
        ring_at = [0]

        def take_bank():
            b = ring_at[0] % RING
            ring_at[0] += 1
            return b

        def transpose(dst, src, ident):
            return lambda e: e.transpose(dst, src, ident)

        def matmul(dst, lhsT, rhs, start, stop):
            return lambda e: e.matmul(dst, lhsT, rhs, start=start, stop=stop)

        def pe_job(bank, calls, waits, s):
            waits = list(waits) + bank_free[bank]
            for n, call in enumerate(calls):
                token = pe.add(call, waits if n == 0 else (), s if n == len(calls) - 1 else None)
            bank_free[bank] = []
            return token

        def chain(calls, first=()):
            token = None
            for call in calls:
                token = dve.add(call, [*first, token], sig["chain"])
                first = ()
            return token

        def ts(o, i, s1, s2, op0, op1=None):
            if op1 is None:
                return lambda e: e.tensor_scalar(o, i, s1, None, op0)
            return lambda e: e.tensor_scalar(o, i, s1, s2, op0, op1)

        def stt(o, i0, s, i1, op0, op1):
            return lambda e: e.scalar_tensor_tensor(out=o, in0=i0, scalar=s, in1=i1, op0=op0, op1=op1)

        def tt(o, a, b, op):
            return lambda e: e.tensor_tensor(o, a, b, op)

        def actv(o, i, f, **kw):
            return lambda e: e.activation(o, i, f, **kw)

        def round_down(o, i):
            return lambda e: e.tensor_scalar(o.bitcast(U32), i.bitcast(U32), EXPONENT, None, ALU.bitwise_and)

        def w(i):
            return ws[:, i:i + 1]

        INV_W = {"k": 0, "q": 1, "v": 2, "o": 3}
        SCALE_W = {"k": 4, "q": 5, "v": 6, "o": 7}
        WMAX = {"k": 8, "q": 9, "v": 10, "o": 11}
        WALL = {"k": 12, "q": 13, "v": 14, "o": 15}
        SUM_PART = {1: 16, 2: 20}
        SUM_ROW, SUM_ALL = {1: 24, 2: 25}, {1: 26, 2: 27}
        ABOVE, BELOW = {1: 28, 2: 29}, {1: 30, 2: 31}
        H_INV, H_SCALE, H_SCALE_Y = 32, 33, 34
        B1_MAX, B1_ALL, TMP = 35, 36, 37

        C = sig["consts"]
        z = pool.add(lambda e: e.memset(ident32[:], 0.0), (), C)
        t_ident = pool.add(lambda e: e.affine_select(
            out=ident32[:], in_=ident32[:], compare_op=ALU.not_equal, fill=1.0, base=0,
            pattern=[[-1, P]], channel_multiplier=1), [z], C)
        t_half = pool.add(lambda e: e.memset(minus_half[:], -0.5), (), C)
        pool.add(lambda e: e.memset(kz_hi[:].rearrange("p a b t -> p (a b t)").bitcast(U32), 0), (), C)
        pool.add(lambda e: e.memset(kz_lo[:].rearrange("p a b t -> p (a b t)").bitcast(U32), 0), (), C)
        t_zero = pool.add(lambda e: e.memset(v1[:, :, :, DV:DV1], 1.0), (), C)
        t_ident16 = dve.add(lambda e: e.tensor_copy(ident16[:], ident32[:]), [t_ident], sig["chain"])

        raw = {n: arena[:, i, :].rearrange("p (k n) -> p k n", k=KT) for i, n in enumerate("kqvo")}
        dram_w = {"k": Wk, "q": Wq, "v": Wv, "o": Wo}

        def group_place(g):
            half, r = divmod(g, LIVE * NSEG)
            seg, live = divmod(r, LIVE)
            return half * LIVE * TG + live * TG, seg, live

        def load_x(g):
            b0, seg, _ = group_place(g)
            src = x[b0:b0 + TG, seg * P:(seg + 1) * P, :].rearrange("b p d -> p b d")
            done["x", g] = sp.add(lambda e: e.dma_start(rows[:, g % NX], src),
                                  after(("out", g - NX, 0), ("out", g - NX, 1)), s_xload[g % NX], 16)

        def load_w(n):
            src = dram_w[n].rearrange("(k p) n -> p k n", p=P)
            done["raw", n] = sp.add(lambda e: e.dma_start(raw[n], src), (), s_wload["kqvo".index(n)], 16)

        def load_ffn_w(m, i):
            if m == 1:
                src = W1.rearrange("(i f p) d -> i p f d", i=4, p=P)[i]
                dst = arena[:, i, :].rearrange("p (f d) -> p f d", d=D)
                waits = after(("wsplit_hi", "kqvo"[i]), ("wsplit_lo", "kqvo"[i]))
            else:
                src = W2.rearrange("(i p) f -> i p f", p=P)[i]
                dst = arena[:, i, :]
                waits = after(("quant", 1, i, 3))
            done["raw", m, i] = sp.add(lambda e: e.dma_start(dst, src), waits, s_wload[i], 16)

        load_w("k")
        load_x(0)
        for n in "qvo":
            load_w(n)
        bt = sp.add(lambda e: e.dma_start(gate_in[:], betas.rearrange("a h b v -> (a b) (h v)")
                                          .rearrange("a n -> (a n)").partition_broadcast(P)),
                    (), sig["bload"], 16)
        sp.add(lambda e: e.dma_start(b2_all[:], b2.partition_broadcast(P)), (), sig["bload"], 16)
        sp.add(lambda e: e.dma_start(b1_rows[:], b1.rearrange("(f p) -> f p", p=P)), (), sig["bload"], 16)
        t_small = (sig["bload"].sem, sig["bload"].count)

        def prepare_w(n):
            t = dve.add(lambda e: e.tensor_reduce(w(WMAX[n]), raw[n], AX_XY, ALU.max,
                                                  apply_absolute_value=True),
                        after(("raw", n)), sig["wmax"])
            t = pool.add(lambda e: e.partition_all_reduce(w(WALL[n]), w(WMAX[n]), P, RMAX), [t], sig["gp_work"])
            t = chain([ts(w(WALL[n]), w(WALL[n]), 2.0 ** -60, None, ALU.max),
                       round_down(w(INV_W[n]), w(WALL[n])),
                       ts(w(INV_W[n]), w(INV_W[n]), 2.0 ** -14, None, ALU.mult),
                       lambda e: e.reciprocal(w(SCALE_W[n]), w(INV_W[n]))], [t])
            t_hi = act.add(actv(w_hi[n][:], raw[n], ACT.Copy, scale=w(SCALE_W[n])), [t], sig["wsplit_hi"])
            t_lo = dve.add(stt(w_lo[n][:].rearrange("p k n -> p (k n)"), raw[n].rearrange("p k n -> p (k n)"),
                               w(SCALE_W[n]), w_hi[n][:].rearrange("p k n -> p (k n)"),
                               ALU.mult, ALU.subtract), [t_hi, t], sig["wsplit_lo"])
            done["wsplit_hi", n], done["wsplit_lo", n] = t_hi, t_lo

        def sum_ffn_w(m, i):
            done["wsum", m, i] = dve.add(
                lambda e: e.tensor_reduce(w(SUM_PART[m] + i), arena[:, i, :], AX_X, ALU.add,
                                          apply_absolute_value=True),
                after(("raw", m, i)), sig["wsum"])

        def threshold(m):
            t = dve.add(lambda e: e.tensor_reduce(w(SUM_ROW[m]), ws[:, SUM_PART[m]:SUM_PART[m] + 4],
                                                  AX_X, ALU.add), after(("wsum", m, 3)), sig["wsum"])
            t = pool.add(lambda e: e.partition_all_reduce(w(SUM_ALL[m]), w(SUM_ROW[m]), P, RADD), [t], sig["gp_work"])
            done["threshold", m] = chain(
                [ts(w(SUM_ALL[m]), w(SUM_ALL[m]), 1.0 / (F * D), EPS, ALU.mult, ALU.add),
                 ts(w(ABOVE[m]), w(SUM_ALL[m]), 0.5, None, ALU.mult),
                 ts(w(BELOW[m]), w(SUM_ALL[m]), -0.5, None, ALU.mult)], [t])

        quant_no = [0]

        def quantise(m, i, b):
            n = quant_no[0]
            quant_no[0] += 1
            s = n % 2
            src = arena[:, i, b * 512:(b + 1) * 512]
            t = dve.add(ts(wbelow[:, s, :], src, w(BELOW[m]), None, ALU.is_lt),
                        after(("threshold", m), ("raw", m, i)), sig["quant"])
            t = dve.add(stt(wquant[:, s, :], src, w(ABOVE[m]), wbelow[:, s, :], ALU.is_gt, ALU.subtract),
                        [t, *after(("wturn", n - 2))], sig["quant"])
            done["quant", m, i, b] = t
            bank = take_bank()
            half = banks[bank][:].bitcast(F16)
            t = pe_job(bank, [transpose(half[:, j * P:(j + 1) * P], wquant[:, s, j * P:(j + 1) * P], ident16[:])
                              for j in range(4)], [t, t_ident16], sig["wturn"])
            done["wturn", n] = t
            src4 = half[:, 0:512].rearrange("p (j c) -> p j c", j=4)
            f0 = (i * 4 + b) * P
            dst = w1t[:, :, f0:f0 + P] if m == 1 else w2t[:, b * 4:b * 4 + 4, i * P:(i + 1) * P]
            done["wput", m] = act.add(actv(dst, src4, ACT.Copy), [t], sig["wput"])
            bank_free[bank] = [done["wput", m]]

        def prepare_ffn_scale():
            bank = take_bank()
            ps = banks[bank][:, 0:FT]
            t = pe_job(bank, [transpose(ps, b1_rows[:], ident32[0:FT, 0:FT])], [t_small, t_ident], sig["wturn"])
            t = dve.add(lambda e: e.tensor_copy(b1_col[:], ps), [t], sig["wmax"])
            bank_free[bank] = [t]
            t = dve.add(lambda e: e.tensor_reduce(w(B1_MAX), b1_col[:], AX_X, ALU.max, apply_absolute_value=True),
                        [t], sig["wmax"])
            t = pool.add(lambda e: e.partition_all_reduce(w(B1_ALL), w(B1_MAX), P, RMAX), [t], sig["gp_work"])
            done["hscale"] = chain(
                [ts(w(B1_ALL), w(B1_ALL), float(D), None, ALU.add),
                 round_down(w(H_INV), w(B1_ALL)),
                 ts(w(H_INV), w(H_INV), 2.0 ** -14, None, ALU.mult),
                 lambda e: e.reciprocal(w(H_SCALE), w(H_INV)),
                 ts(w(H_SCALE_Y), w(H_SCALE), 2.0 ** -9, None, ALU.mult),
                 ts(b1_scaled[:], b1_col[:], w(H_SCALE), None, ALU.mult)], [t])

        def prepare_gates():
            t = act.add(actv(gate_out[:], gate_in[:], ACT.Exp, scale=-1.0), [t_small], sig["actmisc"])
            done["gates"] = chain(
                [ts(gate_out[:], gate_out[:], 1.0, None, ALU.add),
                 lambda e: e.reciprocal(gate_in[:], gate_out[:]),
                 ts(gate_out[:], gate_in[:], -1.0, 1.0, ALU.mult, ALU.add)], [t])

        (G_ALL, G_POW, G_INV, G_SCALE, G_Q, G_K, G_V, G_EXP, G_V11, G_RUN, G_AINV, G_ASCALE, G_WO) = range(13)

        def gcol(g, i):
            return gs[:, g, i:i + 1]

        def group_max(g):
            t = dve.add(lambda e: e.tensor_reduce(amax[:, g % 2:g % 2 + 1], rows[:, g % NX], AX_XY, ALU.max,
                                                  apply_absolute_value=True),
                        after(("x", g)), sig["wmax"])
            done["amax_all", g] = pool.add(
                lambda e: e.partition_all_reduce(gcol(g, G_ALL), amax[:, g % 2:g % 2 + 1], P, RMAX),
                [t], sig["amax_all"])

        def group_x_scale(g):
            done["xscale", g] = chain(
                [ts(gcol(g, G_ALL), gcol(g, G_ALL), 2.0 ** -60, None, ALU.max),
                 round_down(gcol(g, G_POW), gcol(g, G_ALL)),
                 ts(gcol(g, G_INV), gcol(g, G_POW), 2.0 ** -14, None, ALU.mult),
                 lambda e: e.reciprocal(gcol(g, G_SCALE), gcol(g, G_INV))], after(("amax_all", g)))

        def group_scalars(g):
            _, seg, _ = group_place(g)
            before = gcol(g - LIVE, G_POW if seg == 1 else G_RUN) if seg else gcol(g, G_POW)
            done["scal", g] = chain(
                [ts(gcol(g, G_Q), gcol(g, G_INV), w(INV_W["q"]), None, ALU.mult),
                 ts(gcol(g, G_K), gcol(g, G_INV), w(INV_W["k"]), None, ALU.mult),
                 ts(gcol(g, G_V), gcol(g, G_INV), w(INV_W["v"]), None, ALU.mult),
                 ts(gcol(g, G_EXP), gcol(g, G_Q), gcol(g, G_K), DK ** -0.5 * 2.0 ** 48, ALU.mult, ALU.mult),
                 ts(gcol(g, G_V11), gcol(g, G_V), 2.0 ** 11, None, ALU.mult),
                 tt(gcol(g, G_RUN), gcol(g, G_POW), before, ALU.max),
                 ts(gcol(g, G_AINV), gcol(g, G_RUN), w(INV_W["v"]), 2.0 ** 11, ALU.mult, ALU.mult),
                 lambda e: e.reciprocal(gcol(g, G_ASCALE), gcol(g, G_AINV)),
                 ts(gcol(g, G_WO), gcol(g, G_AINV), w(INV_W["o"]), None, ALU.mult)],
                after(("xscale", g), ("wsplit_lo", "o")))

        def split_hi(hi, src, scale, waits, s_hi):
            return act.add(actv(hi, src, ACT.Copy, scale=scale), waits, s_hi)

        def split_lo(hi, lo, src, scale, waits, s_lo):
            return dve.add(stt(lo, src, scale, hi, ALU.mult, ALU.subtract), waits, s_lo)

        def split(bank, hi, lo, src, scale, waits, key, s_hi, s_lo):
            t_hi = split_hi(hi, src, scale, waits, s_hi)
            done[key] = split_lo(hi, lo, src, scale, [t_hi, *waits], s_lo)
            bank_free[bank] += [done[key]]

        def turn_x(g, t):
            bank = take_bank()
            ps = banks[bank][:].rearrange("p (k c) -> p k c", k=KT)
            token = pe_job(bank, [transpose(ps[:, k], rows[:, g % NX, t, k * P:(k + 1) * P], ident32[:])
                                  for k in range(KT)], [t_ident, *after(("x", g))], sig["xturn"])
            split(bank, xt_hi[:, :, t * P:(t + 1) * P], xt_lo[:, :, t * P:(t + 1) * P], ps, gcol(g, G_SCALE),
                  [token, *after(("xscale", g), ("vproj", g - 1, 1))], ("xt", g, t), sig["xt_hi"], sig["xt_lo"])

        def project_qk(g, n, j):
            bank = take_bank()
            ps = banks[bank][:].rearrange("p (c t) -> p c t", c=2)
            calls = []
            for c in range(2):
                cols = slice((2 * j + c) * P, (2 * j + c + 1) * P)
                terms = [(wt[n][:, k, cols], xs[:, k, :]) for k in range(KT)
                         for wt, xs in ((w_hi, xt_hi), (w_hi, xt_lo), (w_lo, xt_hi))]
                calls += [matmul(ps[:, c], a, b, i == 0, i == len(terms) - 1) for i, (a, b) in enumerate(terms)]
            token = pe_job(bank, calls, after(("xt", g, 0), ("xt", g, 1), ("wsplit_lo", n)), sig[n + "proj"])
            pairs = slice(2 * j, 2 * j + 2)
            scored = after(("score", g - 1, 1, 1))
            if n == "q":
                parts = [(q_hi[:, pairs], q_lo[:, pairs], ps)]
            else:
                parts = [(kz_hi[part, pairs, e], kz_lo[part, pairs, e], ps[part])
                         for e, part in enumerate((slice(0, DK), slice(DK, P)))]
            for hi, _, src in parts:
                split_hi(hi, src, 2.0 ** -24, [token, t_zero, *scored], sig["kq_hi"])
            scale = gcol(g, G_Q if n == "q" else G_K)
            flat_ps = banks[bank][:]
            act.add(actv(exp_tmp[:], flat_ps, ACT.Exp, scale=scale), after(("scal", g), "elu"), sig["kq_exp"])
            t_r = act.add(actv(relu_tmp[:], flat_ps, ACT.Relu, scale=scale), (), sig["kq_exp"])
            for hi, lo, src in parts:
                done[n, g, j] = split_lo(hi, lo, src, 2.0 ** -24, [t_r, *scored], sig["kq_lo"])
            bank_free[bank] = [done[n, g, j]]
            dst = (sq_t if n == "q" else sk_t)[:, pairs].rearrange("p c t -> p (c t)")
            waits = after(("num", g - 1, 1)) if n == "q" else after(("skturn", g - 1, 1))
            done["elu"] = done["s" + n, g, j] = dve.add(
                stt(dst, exp_tmp[:], 1.0, relu_tmp[:], ALU.min, ALU.add), [t_r, *waits], sig["kq_sk"])

        def project_v(g, t):
            bank = take_bank()
            toks = slice(t * P, (t + 1) * P)
            terms = [(xs[:, k, toks], wt["v"][:, k, :]) for k in range(KT)
                     for xs, wt in ((xt_hi, w_hi), (xt_hi, w_lo), (xt_lo, w_hi))]
            token = pe_job(bank, [matmul(banks[bank][:], a, b, i == 0, i == len(terms) - 1)
                                  for i, (a, b) in enumerate(terms)],
                           after(("xt", g, t), ("wsplit_lo", "v")), sig["vproj"])
            done["vproj", g, t] = token
            read = after(("pv", g - 1, t))
            split_hi(v_hi[:, t], banks[bank][:], 2.0 ** -24, [token, *read], sig["v_hi"])
            done["v1", g, t] = act.add(
                actv(v1[:, t, :, 0:DV], banks[bank][:].rearrange("p (h v) -> p h v", h=H), ACT.Copy,
                     scale=gcol(g, G_V)), after(("scal", g), ("upd", g - 1, t)), sig["v1"])
            done["v", g, t] = split_lo(v_hi[:, t], v_lo[:, t], banks[bank][:], 2.0 ** -24,
                                       [done["v1", g, t], *read], sig["v_lo"])
            bank_free[bank] = [done["v", g, t]]

        def scores(g, t, half):
            bank = take_bank()
            ps = banks[bank][:].rearrange("p (h t) -> p h t", h=4)
            toks = slice(t * P, (t + 1) * P)
            calls = []
            for i in range(4):
                c, e = 2 * half + i // 2, i % 2
                terms = ((q_hi, kz_hi), (q_hi, kz_lo), (q_lo, kz_hi))
                calls += [matmul(ps[:, i], a[:, c, toks], b[:, c, e, toks], m == 0, m == 2)
                          for m, (a, b) in enumerate(terms)]
            token = pe_job(bank, calls, after(("q", g, half), ("k", g, half)), sig["score"])
            done["score", g, t, half] = token
            hs = slice(4 * half, 4 * half + 4)
            tm = dve.add(lambda e: e.tensor_reduce(row_max[:, t, hs], ps, AX_X, ALU.max),
                         [token], sig["smax"])
            tm = dve.add(ts(exp_bias[:, t, hs], row_max[:, t, hs], gcol(g, G_EXP), -1.0, ALU.mult, ALU.mult),
                         [tm, *after(("scal", g), ("pexp", g - 1, t, half))], sig["smax"])
            for i in range(4):
                h = 4 * half + i
                te = act.add(actv(prob[:, t, h], ps[:, i], ACT.Exp, scale=gcol(g, G_EXP),
                                  bias=exp_bias[:, t, h:h + 1], accum_out=row_sum[:, t, h:h + 1]),
                             [tm, *after(("pturn", g - 1, t, half), ("mix", g - 1, t))], sig["pexp"])
            done["pexp", g, t, half] = te
            bank_free[bank] += [te]

        def turn_p(g, t, half):
            bank = take_bank()
            ps = banks[bank][:].rearrange("p (h t) -> p h t", h=4)
            token = pe_job(bank, [transpose(ps[:, i], prob[:, t, 4 * half + i], ident32[:]) for i in range(4)],
                           after(("pexp", g, t, half)), sig["pturn"])
            done["pturn", g, t, half] = token
            hs = slice(4 * half, 4 * half + 4)
            split(bank, pt_hi[:, t, hs], pt_lo[:, t, hs], ps, 2.0 ** 13, [token, *after(("pv", g - 1, t))],
                  ("pt", g, t, half), sig["pt_hi"], sig["pt_lo"])

        def turn_sk(g, t):
            bank = take_bank()
            token = pe_job(bank, [transpose(banks[bank][:, c * P:(c + 1) * P], sk_t[:, c, t * P:(t + 1) * P], ident32[:])
                                  for c in range(NPAIR)], after(("sk", g, 0), ("sk", g, 1)), sig["skturn"])
            done["skturn", g, t] = token
            done["skrow", g, t] = act.add(actv(sk[:, t], banks[bank][:], ACT.Copy),
                                          [token, *after(("upd", g - 1, t))], sig["sk"])
            bank_free[bank] = [done["skrow", g, t]]

        def reset_memory(live):
            for t in range(TG):
                m = mem[:, live * TG + t]
                token = dve.add(lambda e, m=m: e.memset(m, 0.0), after(("mem", live, t)), sig["mem"])
                dve.add(lambda e, m=m: e.memset(m[0:DK, :, DV:DV1], 1.0 / DK), [token], sig["mem"])
                done["mem", live, t] = dve.add(
                    lambda e, m=m: e.memset(m[DK:P, :, 2 * DV1 - 1:2 * DV1], 1.0 / DK), [token], sig["mem"])

        def read_memory(g, t):
            _, _, live = group_place(g)
            for j in range(2):
                bank = take_bank()
                ps = banks[bank][:, 0:2 * 2 * DV1].rearrange("p (c n) -> p c n", c=2)
                token = pe_job(bank, [matmul(ps[:, c], sq_t[:, 2 * j + c, t * P:(t + 1) * P],
                                             mem[:, live * TG + t, 2 * j + c], True, True) for c in range(2)],
                               after(("sq", g, 0), ("sq", g, 1), ("mem", live, t)), sig["num"])
                heads = ps.rearrange("p c (e n) -> p (c e) n", e=2)
                hs = slice(4 * j, 4 * j + 4)
                td = dve.add(lambda e, o=inv_den[:, t, hs], i=heads[:, :, DV]: e.reciprocal(o, i),
                             [token], sig["den"])
                tm = dve.add(tt(att_mem[:, t, hs], heads[:, :, 0:DV],
                                inv_den[:, t, hs].unsqueeze(2).to_broadcast([P, 4, DV]), ALU.mult),
                             [td, *after(("aturn", g - 1, t))], sig["mix_dve"])
                bank_free[bank] = [tm]
            done["num", g, t] = token
            done["att_mem", g, t] = tm

        def attend(g, t):
            bank = take_bank()
            ps = banks[bank][:].rearrange("p (h v) -> p h v", h=H)
            calls = []
            for h in range(H):
                cols = slice(h * DV, (h + 1) * DV)
                terms = ((pt_hi, v_hi), (pt_hi, v_lo), (pt_lo, v_hi))
                calls += [matmul(ps[:, h], a[:, t, h], b[:, t, cols], m == 0, m == 2)
                          for m, (a, b) in enumerate(terms)]
            token = pe_job(bank, calls, after(("pt", g, t, 0), ("pt", g, t, 1), ("v", g, t)), sig["pv"])
            done["pv", g, t] = token
            ti = dve.add(lambda e: e.reciprocal(inv_sum[:, t], row_sum[:, t]), after(("pexp", g, t, 1)), sig["den"])
            ti = dve.add(ts(dot_scale[:, t], inv_sum[:, t], gcol(g, G_V11), None, ALU.mult),
                         [ti, *after(("scal", g))], sig["den"])
            done["mix", g, t] = ti
            tm = dve.add(tt(att_dot[:, t], ps, dot_scale[:, t].unsqueeze(2).to_broadcast([P, H, DV]), ALU.mult),
                         [token, ti, *after(("mixed", g - 1, t))], sig["mix_dve"])
            bank_free[bank] = [tm]
            a = att_mem[:, t].rearrange("p h v -> p (h v)")
            b = att_dot[:, t].rearrange("p h v -> p (h v)")
            t1 = pool.add(tt(a, a, gate_in[:], ALU.mult), after(("att_mem", g, t), "gates"), sig["mix_pool"])
            t2 = pool.add(tt(b, b, gate_out[:], ALU.mult), [tm], sig["mix_pool"])
            done["mixed", g, t] = pool.add(tt(a, a, b, ALU.add), [t1, t2], sig["mix_pool"])

        def update_memory(g, t):
            _, _, live = group_place(g)
            for j in range(2):
                bank = take_bank()
                ps = banks[bank][:, 0:2 * 2 * DV1].rearrange("p (c n) -> p c n", c=2)
                vv = v1[:, t].rearrange("p (c e) n -> p c (e n)", e=2)
                token = pe_job(bank, [matmul(ps[:, c], sk[:, t, (2 * j + c) * P:(2 * j + c + 1) * P],
                                             vv[:, 2 * j + c], True, True) for c in range(2)],
                               after(("skrow", g, t), ("v1", g, t)), sig["upd"])
                for rs, cs in ((slice(0, DK), slice(0, DV1)), (slice(DK, P), slice(DV1, 2 * DV1))):
                    m = mem[rs, live * TG + t, 2 * j:2 * j + 2, cs]
                    tm = dve.add(tt(m, ps[rs, :, cs], m, ALU.add), [token, *after(("mem", live, t))], sig["mem"])
                bank_free[bank] = [tm]
            done["upd", g, t] = token
            done["mem", live, t] = tm

        def turn_att(g, t):
            bank = take_bank()
            ps = banks[bank][:].rearrange("p (k c) -> p k c", k=KT)
            a = att_mem[:, t].rearrange("p h v -> p (h v)")
            token = pe_job(bank, [transpose(ps[:, k], a[:, k * P:(k + 1) * P], ident32[:]) for k in range(KT)],
                           after(("mixed", g, t)), sig["aturn"])
            done["aturn", g, t] = token
            split(bank, at_hi[:, t], at_lo[:, t], ps, gcol(g, G_ASCALE), [token, *after(("scal", g), ("wo", g - 1, t))],
                  ("at", g, t), sig["at_hi"], sig["at_lo"])

        def layer_stats(g, t, which, waits):
            r = rows[:, g % NX, t]
            ta = dve.add(lambda e: e.bn_stats(stats[:, which, t], r), waits, sig["stat"])
            ta = dve.add(lambda e: e.bn_aggr(mean_var[:, which, t], stats[:, which, t]), [ta], sig["stat"])
            tb = pool.add(lambda e: e.tensor_scalar(var_eps[:, which, t:t + 1], mean_var[:, which, t, 1:2],
                                                    EPS, None, ALU.add), [ta], sig["pow_in"])
            done["rstd", g, t, which] = pool.add(
                tt(rstd[:, which, t:t + 1], var_eps[:, which, t:t + 1], minus_half[:], ALU.pow),
                [tb, t_half], sig["rstd"])

        def normalise(g, t, which):
            r = rows[:, g % NX, t]
            done["norm", g, t, which] = dve.add(
                ts(r, r, mean_var[:, which, t, 0:1], rstd[:, which, t:t + 1], ALU.subtract, ALU.mult),
                after(("rstd", g, t, which)), sig["norm"])

        def project_out(g, t):
            bank = take_bank()
            terms = [(xs[:, t, k], wt["o"][:, k, :]) for k in range(KT)
                     for xs, wt in ((at_hi, w_hi), (at_hi, w_lo), (at_lo, w_hi))]
            token = pe_job(bank, [matmul(banks[bank][:], a, b, i == 0, i == len(terms) - 1)
                                  for i, (a, b) in enumerate(terms)],
                           after(("at", g, t), ("wsplit_lo", "o")), sig["wo"])
            done["wo", g, t] = token
            r = rows[:, g % NX, t]
            tr = dve.add(stt(r, banks[bank][:], gcol(g, G_WO), r, ALU.mult, ALU.add), [token], sig["resid"])
            bank_free[bank] = [tr]
            layer_stats(g, t, 0, [tr])

        def turn_y(g, t):
            bank = take_bank()
            ps = banks[bank][:].rearrange("p (k c) -> p k c", k=KT)
            r = rows[:, g % NX, t]
            token = pe_job(bank, [transpose(ps[:, k], r[:, k * P:(k + 1) * P], ident32[:]) for k in range(KT)],
                           after(("norm", g, t, 0)), sig["yturn"])
            toks = slice(t * P, (t + 1) * P)
            split(bank, yt_hi[:, g % 2, :, toks], yt_lo[:, g % 2, :, toks], ps, 2.0 ** 9,
                  [token, *after(("ffn1", g - 2, 7), ("quant", 2, 3, 3))], ("yt", g, t), sig["yt_hi"], sig["yt_lo"])
            done["yb", g, t] = pool.add(tt(r, r, b2_all[:], ALU.add), [token, t_small], sig["yb"])

        def ffn_up(g, j):
            bank = take_bank()
            ps = banks[bank][:].rearrange("p (c t) -> p c t", c=2)
            calls = []
            for c in range(2):
                cols = slice((2 * j + c) * P, (2 * j + c + 1) * P)
                terms = [(w1t[:, k, cols], ys[:, g % 2, k, :]) for k in range(KT) for ys in (yt_hi, yt_lo)]
                calls += [matmul(ps[:, c], a, b, i == 0, i == len(terms) - 1) for i, (a, b) in enumerate(terms)]
            token = pe_job(bank, calls, after(("yt", g, 0), ("yt", g, 1), ("wput", 1)), sig["ffn1"])
            done["ffn1", g, j] = token
            n = g * 8 + j
            buf = n % NH32
            for c in range(2):
                f = 2 * j + c
                tr = act.add(actv(h32[:, buf, c * GT:(c + 1) * GT], ps[:, c], ACT.Relu, scale=w(H_SCALE_Y),
                                  bias=b1_scaled[:, f:f + 1]),
                             [token, *after("hscale", ("h_lo", n - NH32))], sig["relu"])
            bank_free[bank] = [tr]
            hi = h_hi[:, 2 * j:2 * j + 2].rearrange("p f t -> p (f t)")
            lo = h_lo[:, 2 * j:2 * j + 2].rearrange("p f t -> p (f t)")
            th = dve.add(lambda e: e.tensor_copy(hi, h32[:, buf]), [tr, *after(("ffn2", g - 1, 1))], sig["h_hi"])
            done["h_lo", n] = done["h", g, j] = dve.add(tt(lo, h32[:, buf], hi, ALU.subtract), [th], sig["h_lo"])

        PIECES = 4

        def ffn_down(g, t, piece):
            toks = slice(t * P, (t + 1) * P)
            fs = range(piece * FT // PIECES, (piece + 1) * FT // PIECES)
            terms = [(hs[:, f, toks], w2t[:, f, :], f, hs is h_lo) for f in fs for hs in (h_hi, h_lo)]
            calls = [matmul(banks[7][:], a, b, f == 0 and not is_lo, f == FT - 1 and is_lo)
                     for a, b, f, is_lo in terms]
            last = piece == PIECES - 1
            waits = after(("h", g, fs[-1] // 2), ("wput", 2)) + (bank_free[7] if piece == 0 else [])
            for i, call in enumerate(calls):
                token = pe.add(call, waits if i == 0 else (), sig["ffn2"] if last and i == len(calls) - 1 else None)
            if not last:
                return
            done["ffn2", g, t] = token
            r = rows[:, g % NX, t]
            tr = dve.add(stt(r, banks[7][:], w(H_INV), r, ALU.mult, ALU.add),
                         [token, *after(("yb", g, t), "hscale")], sig["resid"])
            bank_free[7] = [tr]
            layer_stats(g, t, 1, [tr])

        def put_out(g, t):
            normalise(g, t, 1)
            b0, seg, _ = group_place(g)
            done["out", g, t] = sp.add(
                lambda e: e.dma_start(out[b0 + t, seg * P:(seg + 1) * P, :], rows[:, g % NX, t]),
                after(("norm", g, t, 1)), s_xout[g % NX][t], 16)

        def attention_steps(g):
            steps = []

            def step(cost, f, *args):
                steps.append((cost, lambda: f(*args)))

            QK, V, SC, T4 = 24 * 109, 12 * 216, 12 * 56, 4 * 109
            if g + 1 < NG:
                step(0, group_max, g + 1)
            step(QK, project_qk, g, "k", 0)
            step(QK, project_qk, g, "q", 0)
            step(QK, project_qk, g, "k", 1)
            step(SC, scores, g, 0, 0)
            step(QK, project_qk, g, "q", 1)
            step(SC, scores, g, 1, 0)
            step(V, project_v, g, 0)
            step(SC, scores, g, 0, 1)
            step(T4, turn_sk, g, 0)
            step(T4, turn_p, g, 0, 0)
            step(V, project_v, g, 1)
            if g + 1 < NG:
                step(0, group_x_scale, g + 1)
            step(SC, scores, g, 1, 1)
            step(T4, turn_p, g, 0, 1)
            step(4 * 222, read_memory, g, 0)
            step(24 * 34, attend, g, 0)
            step(T4, turn_p, g, 1, 0)
            step(4 * 222, update_memory, g, 0)
            step(T4, turn_sk, g, 1)
            step(4 * 222, read_memory, g, 1)
            step(T4, turn_p, g, 1, 1)
            step(T4, turn_att, g, 0)
            step(24 * 34, attend, g, 1)
            step(4 * 222, update_memory, g, 1)
            step(V, project_out, g, 0)
            if g + 1 < NG:
                step(0, group_scalars, g + 1)
                step(T4, turn_x, g + 1, 0)
            step(T4, turn_att, g, 1)
            step(0, normalise, g, 0, 0)
            if g + 1 < NG:
                step(T4, turn_x, g + 1, 1)
            step(V, project_out, g, 1)
            step(T4, turn_y, g, 0)
            step(0, normalise, g, 1, 0)
            return steps

        def ffn_steps(g):
            steps = [(16 * 109, lambda j=j: ffn_up(g, j)) for j in range(FT // 2)]
            for t in range(TG):
                for piece in range(PIECES):
                    steps.append((8 * 216, lambda t=t, p=piece: ffn_down(g, t, p)))
                    if t == 1 and piece == 0:
                        steps.append((0, lambda: put_out(g, 0)))
            return steps

        def merged(a, b):
            total_a, total_b = sum(c for c, _ in a) or 1, sum(c for c, _ in b) or 1
            at_a = at_b = 0
            a, b = list(a), list(b)
            while a or b:
                if not b or (a and at_a / total_a <= at_b / total_b):
                    cost, f = a.pop(0)
                    at_a += cost
                else:
                    cost, f = b.pop(0)
                    at_b += cost
                f()

        prepare_w("k")
        group_max(0)
        group_x_scale(0)
        prepare_w("q")
        turn_x(0, 0)
        turn_x(0, 1)
        prepare_w("v")
        prepare_w("o")
        group_scalars(0)
        for i in range(4):
            load_ffn_w(1, i)
        load_x(1)
        for live in range(LIVE):
            reset_memory(live)
        prepare_gates()
        prepare_ffn_scale()

        prep = []
        for m in (1, 2):
            for i in range(4):
                prep.append((500, lambda m=m, i=i: sum_ffn_w(m, i)))
            prep.append((500, lambda m=m: threshold(m)))
            for i in range(4):
                for b in range(4):
                    prep.append((500, lambda m=m, i=i, b=b: quantise(m, i, b)))
                if m == 1:
                    prep.append((0, lambda i=i: load_ffn_w(2, i)))
        merged(attention_steps(0)[:-2], prep)
        attention_tail = attention_steps(0)[-2:]
        for _, f in attention_tail:
            f()

        for g in range(1, NG + 1):
            if g + 1 < NG:
                load_x(g + 1)
            if g < NG and g % (LIVE * NSEG) < LIVE and g >= LIVE * NSEG:
                reset_memory(group_place(g)[2])
            turn_y(g - 1, 1)
            merged(attention_steps(g) if g < NG else [], ffn_steps(g - 1))
            put_out(g - 1, 1)

        sp.add(None, [(s.sem, s.count) for pair in s_xout for s in pair])

        block = ctx.enter_context(nc.Block())

        @block.sync
        def _(eng):
            sp.replay(eng)

        @block.tensor
        def _(eng):
            pe.replay(eng)

        @block.vector
        def _(eng):
            dve.replay(eng)

        @block.scalar
        def _(eng):
            act.replay(eng)

        @block.gpsimd
        def _(eng):
            pool.replay(eng)


_INS = ["L0_attn_x", "L0_attn_Wq", "L0_attn_Wk", "L0_attn_Wv", "L0_attn_betas", "L0_attn_Wo",
        "L0_ffn_W1", "L0_ffn_b1", "L0_ffn_W2", "L0_ffn_b2"]


def kernel(**inputs):
    import numpy as np
    import concourse.bacc as bacc
    from concourse.bass_utils import run_bass_kernel_spmd

    nc = bacc.Bacc("TRN2", target_bir_lowering=False, num_devices=1)
    arrays, args = {}, []
    for name in _INS:
        a = np.ascontiguousarray(inputs[name])
        arrays[f"in_{name}"] = a
        args.append(nc.dram_tensor(f"in_{name}", a.shape, mybir.dt.from_np(a.dtype), kind="ExternalInput").ap())
    shape = inputs["L0_attn_x"].shape
    args.append(nc.dram_tensor("out_rows", shape, F32, kind="ExternalOutput").ap())
    build_program(nc, *args)
    result = run_bass_kernel_spmd(nc, [arrays], core_ids=[0])
    return result.results[0]["out_rows"]
```

```python
from contextlib import ExitStack

import concourse.bass as bass
import concourse.mybir as mybir

ALU = mybir.AluOpType
ACT = mybir.ActivationFunctionType
F32 = mybir.dt.float32
F16 = mybir.dt.float16
U32 = mybir.dt.uint32
AX_X = mybir.AxisListType.X
AX_XY = mybir.AxisListType.XY
RMAX = bass.bass_isa.ReduceOp.max
RADD = bass.bass_isa.ReduceOp.add

P = 128
RING = 6
EXPONENT = 0x7F800000
EPS = 1e-5


TURN = (
    "update1 max k0 turn_y0 q0 attend1 k1 turn_att1 xscale0 q1 v0 score00 out1 score11 "
    "score10 xscale1 norm1 xscale2 score01 turn_y1 v1 sums00 turn_p00 turn_sk0",
    "turn_p01 norm_end turn_sk1 xscale3 put_end load sums01 scalars0 read0 attend0 scalars1 "
    "read1 turn_p10 sums10 turn_p11 turn_x0 update0 sums11 scalars2 turn_att0 turn_x1 out0 "
    "norm0",
)

EARLY = 6


class Signal:

    def __init__(self, sem):
        self.sem = sem
        self.count = 0


class Queue:

    def __init__(self):
        self.items = []
        self.waited = {}

    def add(self, emit, after=(), signal=None, by=1):
        waits = []
        for token in after:
            if token is None:
                continue
            sem, value = token
            if self.waited.get(id(sem), 0) < value:
                self.waited[id(sem)] = value
                waits.append(token)
        if signal is not None:
            signal.count += by
        self.items.append((waits, emit, signal.sem if signal else None, by))
        return (signal.sem, signal.count) if signal else None

    def replay(self, eng):
        for waits, emit, sem, by in self.items:
            for s, value in waits:
                eng.wait_ge(s, value)
            ins = emit(eng) if emit else None
            if sem is not None:
                ins.then_inc(sem, by)


def build_program(nc, x, Wq, Wk, Wv, betas, Wo, W1, b1, W2, b2, out):
    B, S, D = x.shape
    H, DV = betas.shape[1], betas.shape[3]
    DK = Wq.shape[1] // H
    F = W1.shape[0]
    KT = D // P
    FT = F // P
    NPAIR = H * DK // P
    NSEG = S // P
    TG = 2
    GT = TG * P
    LIVE = 2
    NG = B // TG * NSEG
    DV1 = DV + 1
    assert DK == DV == 64 and D == 512 and H == 8 and B % (TG * LIVE) == 0 and S % P == 0

    ctx = ExitStack()
    with ctx:
        def sb(name, shape, dt=F32):
            return ctx.enter_context(nc.sbuf_tensor(name, shape, dt))

        def signal(name):
            return Signal(ctx.enter_context(nc.semaphore(name)))

        banks = [ctx.enter_context(nc.psum_tensor(f"bank{i}", [P, 512], F32)) for i in range(8)]

        w_hi = {n: sb(f"w{n}_hi", [P, KT, D], F16) for n in "kqvo"}
        w_lo = {n: sb(f"w{n}_lo", [P, KT, D], F16) for n in "kqvo"}
        w1t = sb("w1t", [P, KT, F], F16)
        w2t = sb("w2t", [P, FT, D], F16)
        arena = sb("arena", [P, 4, 2048], F32)
        ident32 = sb("ident32", [P, P])
        ident16 = sb("ident16", [P, P], F16)
        minus16 = sb("minus16", [P, P], F16)
        gate_in = sb("gate_in", [P, D])
        gate_out = sb("gate_out", [P, D])
        b2_all = sb("b2_all", [P, D])
        b1_col = sb("b1_col", [P, FT])
        b1_rows = sb("b1_rows", [FT, P])
        b1_scaled = sb("b1_scaled", [P, FT])
        minus_half = sb("minus_half", [P, 1])
        ws = sb("wscalars", [P, 40])
        gs = sb("gscalars", [P, NG, 16])

        NX = 4
        rows = sb("rows", [P, NX, TG, D])
        xt_hi = sb("xt_hi", [P, KT, GT], F16)
        xt_lo = sb("xt_lo", [P, KT, GT], F16)
        q_both = sb("q_both", [P, NPAIR, 2, GT], F16)
        k_hi = sb("k_hi", [P, NPAIR, 2, GT], F16)
        k_lo = sb("k_lo", [P, NPAIR, 2, GT], F16)
        sq_t = sb("sq_t", [P, NPAIR, GT])
        sk_t = sb("sk_t", [P, NPAIR, GT])
        exp_tmp = sb("exp_tmp", [P, 512])
        relu_tmp = sb("relu_tmp", [P, 512])
        v_hi = sb("v_hi", [P, TG, D], F16)
        v_lo = sb("v_lo", [P, TG, D], F16)
        v1 = sb("v1", [P, TG, H, DV1])
        sk = sb("sk", [P, TG, H * DK])
        prob = sb("prob", [P, TG, H, P])
        pt_hi = sb("pt_hi", [P, TG, H, P], F16)
        pt_lo = sb("pt_lo", [P, TG, H, P], F16)
        att_mem = sb("att_mem", [P, TG, H, DV])
        att_dot = sb("att_dot", [P, TG, H, DV])
        at_hi = sb("at_hi", [P, TG, KT, P], F16)
        at_lo = sb("at_lo", [P, TG, KT, P], F16)
        mem = sb("mem", [P, LIVE * TG, NPAIR, 2 * DV1])
        row_max = sb("row_max", [P, TG, H])
        exp_bias = sb("exp_bias", [P, TG, H])
        row_sum = sb("row_sum", [P, TG, H])
        inv_sum = sb("inv_sum", [P, TG, H])
        dot_scale = sb("dot_scale", [P, TG, H])
        inv_den = sb("inv_den", [P, TG, H])
        amax = sb("amax", [P, 2])
        stats = sb("stats", [P, 2, TG, 6])
        mean_var = sb("mean_var", [P, 2, TG, 2])
        var_eps = sb("var_eps", [P, 2, TG])
        rstd = sb("rstd", [P, 2, TG])

        flat = arena[:].rearrange("p a b -> p (a b)")
        h_hi = flat[:, 0:2048].bitcast(F16).rearrange("p (f t) -> p f t", f=FT)
        h_lo = flat[:, 2048:4096].bitcast(F16).rearrange("p (f t) -> p f t", f=FT)
        NH32 = 4
        h32 = flat[:, 4096:4096 + NH32 * 512].rearrange("p (b t) -> p b t", b=NH32)
        yt_hi = sb("yt_hi", [P, 2, KT, GT], F16)
        yt_lo = sb("yt_lo", [P, 2, KT, GT], F16)
        wabove = yt_hi[:, 1].rearrange("p k t -> p (k t)").rearrange("p (b n) -> p b n", b=2)
        wbelow = yt_lo[:, 1].rearrange("p k t -> p (k t)").rearrange("p (b n) -> p b n", b=2)

        names = ("consts gp_work bload "
                 "wmax wsum scal wsplit_hi wsplit_lo quant wturn wput amax_all "
                 "xturn xt_hi xt_lo kproj qproj vproj kq_hi kq_lo kq_exp kq_sk v_hi v_lo v1 "
                 "score smax pexp pturn pt_hi pt_lo pv num skturn sk upd mem den mix_dve mix_pool "
                 "aturn at_hi at_lo wo resid stat pow_in rstd norm yturn yt_hi yt_lo yb "
                 "ffn1 relu h_hi h_lo h_lo_pool ffn2 chain actmisc")
        sig = {n: signal("s_" + n) for n in names.split()}

        s_wload = [signal(f"s_wload{i}") for i in range(4)]
        s_xload = [signal(f"s_xload{i}") for i in range(NX)]
        s_xout = [[signal(f"s_xout{i}_{t}") for t in range(TG)] for i in range(NX)]

        pe, act, dve, pool, sp = (Queue() for _ in range(5))
        done = {}

        def after(*keys):
            return [done.get(k) for k in keys]

        bank_free = [[] for _ in range(8)]
        ring_at = [0]

        def take_bank():
            b = ring_at[0] % RING
            ring_at[0] += 1
            return b

        def transpose(dst, src, ident):
            return lambda e: e.transpose(dst, src, ident)

        def matmul(dst, lhsT, rhs, start, stop):
            return lambda e: e.matmul(dst, lhsT, rhs, start=start, stop=stop)

        def pe_job(bank, calls, waits, s):
            waits = list(waits) + bank_free[bank]
            for n, call in enumerate(calls):
                token = pe.add(call, waits if n == 0 else (), s if n == len(calls) - 1 else None)
            bank_free[bank] = []
            return token

        def chain(calls, first=()):
            token = None
            for call in calls:
                token = dve.add(call, [*first, token], sig["chain"])
                first = ()
            return token

        def ts(o, i, s1, s2, op0, op1=None):
            if op1 is None:
                return lambda e: e.tensor_scalar(o, i, s1, None, op0)
            return lambda e: e.tensor_scalar(o, i, s1, s2, op0, op1)

        def stt(o, i0, s, i1, op0, op1):
            return lambda e: e.scalar_tensor_tensor(out=o, in0=i0, scalar=s, in1=i1, op0=op0, op1=op1)

        def tt(o, a, b, op):
            return lambda e: e.tensor_tensor(o, a, b, op)

        def actv(o, i, f, **kw):
            return lambda e: e.activation(o, i, f, **kw)

        def round_down(o, i):
            return lambda e: e.tensor_scalar(o.bitcast(U32), i.bitcast(U32), EXPONENT, None, ALU.bitwise_and)

        def w(i):
            return ws[:, i:i + 1]

        INV_W = {"k": 0, "q": 1, "v": 2, "o": 3}
        SCALE_W = {"k": 4, "q": 5, "v": 6, "o": 7}
        WMAX = {"k": 8, "q": 9, "v": 10, "o": 11}
        WALL = {"k": 12, "q": 13, "v": 14, "o": 15}
        SUM_PART = {1: 16, 2: 20}
        SUM_ROW, SUM_ALL = {1: 24, 2: 25}, {1: 26, 2: 27}
        ABOVE, BELOW = {1: 28, 2: 29}, {1: 30, 2: 31}
        H_INV, H_SCALE, H_SCALE_Y = 32, 33, 34
        B1_MAX, B1_ALL, TMP = 35, 36, 37

        C = sig["consts"]
        z = pool.add(lambda e: e.memset(ident32[:], 0.0), (), C)
        t_ident = pool.add(lambda e: e.affine_select(
            out=ident32[:], in_=ident32[:], compare_op=ALU.not_equal, fill=1.0, base=0,
            pattern=[[-1, P]], channel_multiplier=1), [z], C)
        t_half = pool.add(lambda e: e.memset(minus_half[:], -0.5), (), C)
        pool.add(lambda e: e.memset(k_lo[:].rearrange("p a b t -> p (a b t)").bitcast(U32), 0), (), C)
        t_zero = pool.add(lambda e: e.memset(v1[:, :, :, DV:DV1], 1.0), (), C)
        dve.add(lambda e: e.tensor_copy(ident16[:], ident32[:]), [t_ident], sig["chain"])
        t_ident16 = dve.add(ts(minus16[:], ident32[:], -1.0, None, ALU.mult), (), sig["chain"])

        raw = {n: arena[:, i, :].rearrange("p (k n) -> p k n", k=KT) for i, n in enumerate("kqvo")}
        dram_w = {"k": Wk, "q": Wq, "v": Wv, "o": Wo}

        def group_place(g):
            half, r = divmod(g, LIVE * NSEG)
            seg, live = divmod(r, LIVE)
            return half * LIVE * TG + live * TG, seg, live

        def load_x(g):
            b0, seg, _ = group_place(g)
            src = x[b0:b0 + TG, seg * P:(seg + 1) * P, :].rearrange("b p d -> p b d")
            done["x", g] = sp.add(lambda e: e.dma_start(rows[:, g % NX], src),
                                  after(("out", g - NX, 0), ("out", g - NX, 1),
                                        *([("wsum", 2, 3)] if g == NX - 1 else [])), s_xload[g % NX], 16)

        def load_w(n):
            src = dram_w[n].rearrange("(k p) n -> p k n", p=P)
            done["raw", n] = sp.add(lambda e: e.dma_start(raw[n], src), (), s_wload["kqvo".index(n)], 16)

        def load_ffn_w(m, i):
            if m == 1:
                src = W1.rearrange("(i f p) d -> i p f d", i=4, p=P)[i]
                dst = arena[:, i, :].rearrange("p (f d) -> p f d", d=D)
                waits = after(("wsplit_hi", "kqvo"[i]), ("wsplit_lo", "kqvo"[i]))
            else:
                src = W2.rearrange("(i p) f -> i p f", p=P)[i]
                dst = arena[:, i, :]
                waits = after(("quant", 1, i))
            done["raw", m, i] = sp.add(lambda e: e.dma_start(dst, src), waits, s_wload[i], 16)

        load_x(0)
        load_w("k")
        for n in "qvo":
            load_w(n)
        bt = sp.add(lambda e: e.dma_start(gate_in[:], betas.rearrange("a h b v -> (a b) (h v)")
                                          .rearrange("a n -> (a n)").partition_broadcast(P)),
                    (), sig["bload"], 16)
        sp.add(lambda e: e.dma_start(b2_all[:], b2.partition_broadcast(P)), (), sig["bload"], 16)
        sp.add(lambda e: e.dma_start(b1_rows[:], b1.rearrange("(f p) -> f p", p=P)), (), sig["bload"], 16)
        t_small = (sig["bload"].sem, sig["bload"].count)

        def scale_w(n):
            t = dve.add(lambda e: e.tensor_reduce(w(WMAX[n]), raw[n], AX_XY, ALU.max,
                                                  apply_absolute_value=True),
                        after(("raw", n)), sig["wmax"])
            t = pool.add(lambda e: e.partition_all_reduce(w(WALL[n]), w(WMAX[n]), P, RMAX), [t], sig["gp_work"])
            done["wscale", n] = chain(
                [ts(w(WALL[n]), w(WALL[n]), 2.0 ** -60, None, ALU.max),
                 round_down(w(INV_W[n]), w(WALL[n])),
                 ts(w(INV_W[n]), w(INV_W[n]), 2.0 ** -14, None, ALU.mult),
                 lambda e: e.reciprocal(w(SCALE_W[n]), w(INV_W[n]))], [t])

        def split_w(n):
            t = done["wscale", n]
            t_hi = act.add(actv(w_hi[n][:], raw[n], ACT.Copy, scale=w(SCALE_W[n])), [t], sig["wsplit_hi"])
            lo, hi, full = (a.rearrange("p k n -> p (k n)") for a in (w_lo[n][:], w_hi[n][:], raw[n]))
            done["wsplit_hi", n] = t_hi
            done["wsplit_lo", n] = dve.add(stt(lo, full, w(SCALE_W[n]), hi, ALU.mult, ALU.subtract),
                                           [t_hi, t], sig["wsplit_lo"])

        unread = rows[:, NX - 1].rearrange("p t d -> p (t d)").bitcast(mybir.dt.bfloat16)

        def sum_ffn_w(m, i):
            done["wsum", m, i] = act.add(
                actv(unread, arena[:, i, :], ACT.Abs, accum_out=w(SUM_PART[m] + i)),
                after(("raw", m, i), "unread"), sig["wsum"])
            done["unread"] = done["wsum", m, i]

        def threshold(m):
            t = dve.add(lambda e: e.tensor_reduce(w(SUM_ROW[m]), ws[:, SUM_PART[m]:SUM_PART[m] + 4],
                                                  AX_X, ALU.add), after(("wsum", m, 3)), sig["wmax"])
            t = pool.add(lambda e: e.partition_all_reduce(w(SUM_ALL[m]), w(SUM_ROW[m]), P, RADD), [t], sig["gp_work"])
            done["threshold", m] = chain(
                [ts(w(SUM_ALL[m]), w(SUM_ALL[m]), 1.0 / (F * D), EPS, ALU.mult, ALU.add),
                 ts(w(ABOVE[m]), w(SUM_ALL[m]), 0.5, None, ALU.mult),
                 ts(w(BELOW[m]), w(SUM_ALL[m]), -0.5, None, ALU.mult)], [t])

        def compare(m, i, b):
            n = ((m - 1) * 4 + i) * 4 + b
            src = arena[:, i, b * 512:(b + 1) * 512]
            waits = after(("threshold", m), ("raw", m, i), ("wturn", n - 2))
            dve.add(ts(wabove[:, n % 2, :], src, w(ABOVE[m]), None, ALU.is_gt), waits, sig["quant"])
            done["quant", n] = done["quant", m, i] = dve.add(
                ts(wbelow[:, n % 2, :], src, w(BELOW[m]), None, ALU.is_lt), (), sig["quant"])

        def turn_w(m, i, b):
            n = ((m - 1) * 4 + i) * 4 + b
            bank = take_bank()
            ps = banks[bank][:].rearrange("p (j c) -> p j c", j=4)
            calls = []
            for j in range(4):
                cols = slice(j * P, (j + 1) * P)
                calls += [matmul(ps[:, j], wabove[:, n % 2, cols], ident16[:], True, False),
                          matmul(ps[:, j], wbelow[:, n % 2, cols], minus16[:], False, True)]
            t = pe_job(bank, calls, [t_ident16, *after(("quant", n))], sig["wturn"])
            done["wturn", n] = t
            f0 = (i * 4 + b) * P
            dst = w1t[:, :, f0:f0 + P] if m == 1 else w2t[:, b * 4:b * 4 + 4, i * P:(i + 1) * P]
            done["wput", m] = act.add(actv(dst, ps, ACT.Copy), [t], sig["wput"])
            bank_free[bank] = [done["wput", m]]

        def prepare_ffn_scale():
            bank = take_bank()
            ps = banks[bank][:, 0:FT]
            t = pe_job(bank, [transpose(ps, b1_rows[:], ident32[0:FT, 0:FT])], [t_small, t_ident], sig["wturn"])
            t = dve.add(lambda e: e.tensor_copy(b1_col[:], ps), [t], sig["wmax"])
            bank_free[bank] = [t]
            t = dve.add(lambda e: e.tensor_reduce(w(B1_MAX), b1_col[:], AX_X, ALU.max, apply_absolute_value=True),
                        [t], sig["wmax"])
            t = pool.add(lambda e: e.partition_all_reduce(w(B1_ALL), w(B1_MAX), P, RMAX), [t], sig["gp_work"])
            done["hscale"] = chain(
                [ts(w(B1_ALL), w(B1_ALL), float(D), None, ALU.add),
                 round_down(w(H_INV), w(B1_ALL)),
                 ts(w(H_INV), w(H_INV), 2.0 ** -14, None, ALU.mult),
                 lambda e: e.reciprocal(w(H_SCALE), w(H_INV)),
                 ts(w(H_SCALE_Y), w(H_SCALE), 2.0 ** -9, None, ALU.mult),
                 ts(b1_scaled[:], b1_col[:], w(H_SCALE), None, ALU.mult)], [t])

        def prepare_gates():
            t = act.add(actv(gate_out[:], gate_in[:], ACT.Exp, scale=-1.0), [t_small], sig["actmisc"])
            done["gates"] = chain(
                [ts(gate_out[:], gate_out[:], 1.0, None, ALU.add),
                 lambda e: e.reciprocal(gate_in[:], gate_out[:]),
                 ts(gate_out[:], gate_in[:], -1.0, 1.0, ALU.mult, ALU.add)], [t])

        (G_ALL, G_POW, G_INV, G_SCALE, G_Q, G_K, G_V, G_EXP, G_V11, G_RUN, G_AINV, G_ASCALE, G_WO) = range(13)

        def gcol(g, i):
            return gs[:, g, i:i + 1]

        def group_max(g):
            t = dve.add(lambda e: e.tensor_reduce(amax[:, g % 2:g % 2 + 1], rows[:, g % NX], AX_XY, ALU.max,
                                                  apply_absolute_value=True),
                        after(("x", g)), sig["wmax"])
            done["amax_all", g] = pool.add(
                lambda e: e.partition_all_reduce(gcol(g, G_ALL), amax[:, g % 2:g % 2 + 1], P, RMAX),
                [t], sig["amax_all"])

        def side_by_side(calls, waits, key):
            for i, call in enumerate(calls):
                done[key] = dve.add(call, waits if i == 0 else (), sig["scal"])

        def group_x_scale(g, level):
            call, before = [
                (ts(gcol(g, G_ALL), gcol(g, G_ALL), 2.0 ** -60, None, ALU.max), ("amax_all", g)),
                (round_down(gcol(g, G_POW), gcol(g, G_ALL)), ("xclamp", g)),
                (ts(gcol(g, G_INV), gcol(g, G_POW), 2.0 ** -14, None, ALU.mult), ("xpow", g)),
                (lambda e: e.reciprocal(gcol(g, G_SCALE), gcol(g, G_INV)), ("xinv", g))][level]
            side_by_side([call], after(before), (("xclamp", "xpow", "xinv", "xscale")[level], g))

        def group_scalars(g, level):
            _, seg, _ = group_place(g)
            before = gcol(g - LIVE, G_POW if seg == 1 else G_RUN) if seg else gcol(g, G_POW)
            if level == 0:
                side_by_side(
                    [ts(gcol(g, G_Q), gcol(g, G_INV), w(INV_W["q"]), None, ALU.mult),
                     ts(gcol(g, G_K), gcol(g, G_INV), w(INV_W["k"]), None, ALU.mult),
                     ts(gcol(g, G_V), gcol(g, G_INV), w(INV_W["v"]), None, ALU.mult),
                     tt(gcol(g, G_RUN), gcol(g, G_POW), before, ALU.max)],
                    after(("xscale", g), ("wsplit_lo", "v")), ("scal0", g))
            elif level == 1:
                side_by_side(
                    [ts(gcol(g, G_EXP), gcol(g, G_Q), gcol(g, G_K), DK ** -0.5 * 2.0 ** 48, ALU.mult, ALU.mult),
                     ts(gcol(g, G_V11), gcol(g, G_V), 2.0 ** 11, None, ALU.mult),
                     ts(gcol(g, G_AINV), gcol(g, G_RUN), w(INV_W["v"]), 2.0 ** 11, ALU.mult, ALU.mult)],
                    after(("scal0", g)), ("scal", g))
            else:
                side_by_side(
                    [lambda e: e.reciprocal(gcol(g, G_ASCALE), gcol(g, G_AINV)),
                     ts(gcol(g, G_WO), gcol(g, G_AINV), w(INV_W["o"]), None, ALU.mult)],
                    after(("scal", g), ("wsplit_lo", "o")), ("outscal", g))

        def split_hi(hi, src, scale, waits, s_hi):
            return act.add(actv(hi, src, ACT.Copy, scale=scale), waits, s_hi)

        def split_lo(hi, lo, src, scale, waits, s_lo):
            return dve.add(stt(lo, src, scale, hi, ALU.mult, ALU.subtract), waits, s_lo)

        def split(bank, hi, lo, src, scale, waits, key, s_hi, s_lo):
            t_hi = split_hi(hi, src, scale, waits, s_hi)
            done[key] = split_lo(hi, lo, src, scale, [t_hi, *waits], s_lo)
            bank_free[bank] += [done[key]]

        def turn_x(g, t):
            bank = take_bank()
            ps = banks[bank][:].rearrange("p (k c) -> p k c", k=KT)
            token = pe_job(bank, [transpose(ps[:, k], rows[:, g % NX, t, k * P:(k + 1) * P], ident32[:])
                                  for k in range(KT)], [t_ident, *after(("x", g))], sig["xturn"])
            split(bank, xt_hi[:, :, t * P:(t + 1) * P], xt_lo[:, :, t * P:(t + 1) * P], ps, gcol(g, G_SCALE),
                  [token, *after(("xscale", g), ("vproj", g - 1, 1))], ("xt", g, t), sig["xt_hi"], sig["xt_lo"])

        def project_qk(g, n, j):
            bank = take_bank()
            ps = banks[bank][:].rearrange("p (c t) -> p c t", c=2)
            calls = []
            for c in range(2):
                cols = slice((2 * j + c) * P, (2 * j + c + 1) * P)
                terms = [(wt[n][:, k, cols], xs[:, k, :]) for k in range(KT)
                         for wt, xs in ((w_hi, xt_hi), (w_hi, xt_lo), (w_lo, xt_hi))]
                calls += [matmul(ps[:, c], a, b, i == 0, i == len(terms) - 1) for i, (a, b) in enumerate(terms)]
            token = pe_job(bank, calls, after(("xt", g, 0), ("xt", g, 1), ("wsplit_lo", n)), sig[n + "proj"])
            pairs = slice(2 * j, 2 * j + 2)
            scored = after(("score", g - 1, 1, 1))
            halves = (slice(0, DK), slice(DK, P))
            for e, own in enumerate(halves):
                dst = q_both if n == "q" else k_hi
                split_hi(dst[own, pairs, e], ps[own], 2.0 ** -24, [token, t_zero, *scored], sig["kq_hi"])
            scale = gcol(g, G_Q if n == "q" else G_K)
            flat_ps = banks[bank][:]
            act.add(actv(exp_tmp[:], flat_ps, ACT.Exp, scale=scale), after(("scal", g), "elu"), sig["kq_exp"])
            t_r = act.add(actv(relu_tmp[:], flat_ps, ACT.Relu, scale=scale), (), sig["kq_exp"])
            for e, own in enumerate(halves):
                other = halves[1 - e]
                if n == "q":
                    t_lo = split_lo(q_both[own, pairs, e], q_both[other, pairs, e], ps[own], 2.0 ** -24,
                                    [t_r, *scored], sig["kq_lo"])
                else:
                    t_lo = split_lo(k_hi[own, pairs, e], k_lo[own, pairs, e], ps[own], 2.0 ** -24,
                                    [t_r, *scored], sig["kq_lo"])
            bank_free[bank] = [t_lo]
            done[n, g, j] = t_lo
            if n == "k":
                for e, own in enumerate(halves):
                    done[n, g, j] = dve.add(
                        lambda eng, e=e, a=own, b=halves[1 - e]: eng.tensor_copy(k_hi[b, pairs, e], k_hi[a, pairs, e]),
                        (), sig["kq_lo"])
            dst = (sq_t if n == "q" else sk_t)[:, pairs].rearrange("p c t -> p (c t)")
            waits = after(("num", g - 1, 1)) if n == "q" else after(("skturn", g - 1, 1))
            done["elu"] = done["s" + n, g, j] = dve.add(
                stt(dst, exp_tmp[:], 1.0, relu_tmp[:], ALU.min, ALU.add), [t_r, *waits], sig["kq_sk"])

        def project_v(g, t):
            bank = take_bank()
            toks = slice(t * P, (t + 1) * P)
            terms = [(xs[:, k, toks], wt["v"][:, k, :]) for k in range(KT)
                     for xs, wt in ((xt_hi, w_hi), (xt_hi, w_lo), (xt_lo, w_hi))]
            token = pe_job(bank, [matmul(banks[bank][:], a, b, i == 0, i == len(terms) - 1)
                                  for i, (a, b) in enumerate(terms)],
                           after(("xt", g, t), ("wsplit_lo", "v")), sig["vproj"])
            done["vproj", g, t] = token
            read = after(("pv", g - 1, t))
            split_hi(v_hi[:, t], banks[bank][:], 2.0 ** -24, [token, *read], sig["v_hi"])
            done["v1", g, t] = act.add(
                actv(v1[:, t, :, 0:DV], banks[bank][:].rearrange("p (h v) -> p h v", h=H), ACT.Copy,
                     scale=gcol(g, G_V)), after(("scal", g), ("upd", g - 1, t)), sig["v1"])
            done["v", g, t] = split_lo(v_hi[:, t], v_lo[:, t], banks[bank][:], 2.0 ** -24,
                                       [done["v1", g, t], *read], sig["v_lo"])
            bank_free[bank] = [done["v", g, t]]

        def scores(g, t, half):
            bank = take_bank()
            ps = banks[bank][:].rearrange("p (h t) -> p h t", h=4)
            toks = slice(t * P, (t + 1) * P)
            calls = []
            for i in range(4):
                c, e = 2 * half + i // 2, i % 2
                calls += [matmul(ps[:, i], q_both[:, c, e, toks], k_hi[:, c, e, toks], True, False),
                          matmul(ps[:, i], q_both[:, c, e, toks], k_lo[:, c, e, toks], False, True)]
            token = pe_job(bank, calls, after(("q", g, half), ("k", g, half)), sig["score"])
            done["score", g, t, half] = token
            hs = slice(4 * half, 4 * half + 4)
            tm = dve.add(lambda e: e.tensor_reduce(row_max[:, t, hs], ps, AX_X, ALU.max),
                         [token], sig["smax"])
            tm = dve.add(ts(exp_bias[:, t, hs], row_max[:, t, hs], gcol(g, G_EXP), -1.0, ALU.mult, ALU.mult),
                         [tm, *after(("scal", g), ("pexp", g - 1, t, half))], sig["smax"])
            for i in range(4):
                h = 4 * half + i
                te = act.add(actv(prob[:, t, h], ps[:, i], ACT.Exp, scale=gcol(g, G_EXP),
                                  bias=exp_bias[:, t, h:h + 1], accum_out=row_sum[:, t, h:h + 1]),
                             [tm, *after(("pturn", g - 1, t, half), ("mix", g - 1, t))], sig["pexp"])
            done["pexp", g, t, half] = te
            bank_free[bank] += [te]

        def turn_p(g, t, half):
            bank = take_bank()
            ps = banks[bank][:].rearrange("p (h t) -> p h t", h=4)
            token = pe_job(bank, [transpose(ps[:, i], prob[:, t, 4 * half + i], ident32[:]) for i in range(4)],
                           after(("pexp", g, t, half)), sig["pturn"])
            done["pturn", g, t, half] = token
            hs = slice(4 * half, 4 * half + 4)
            split(bank, pt_hi[:, t, hs], pt_lo[:, t, hs], ps, 2.0 ** 13, [token, *after(("pv", g - 1, t))],
                  ("pt", g, t, half), sig["pt_hi"], sig["pt_lo"])

        def turn_sk(g, t):
            bank = take_bank()
            token = pe_job(bank, [transpose(banks[bank][:, c * P:(c + 1) * P], sk_t[:, c, t * P:(t + 1) * P], ident32[:])
                                  for c in range(NPAIR)], after(("sk", g, 0), ("sk", g, 1)), sig["skturn"])
            done["skturn", g, t] = token
            done["skrow", g, t] = act.add(actv(sk[:, t], banks[bank][:], ACT.Copy),
                                          [token, *after(("upd", g - 1, t))], sig["sk"])
            bank_free[bank] = [done["skrow", g, t]]

        def reset_memory(live):
            for t in range(TG):
                m = mem[:, live * TG + t]
                token = pool.add(lambda e, m=m: e.memset(m, 0.0), after(("mem", live, t)), sig["gp_work"])
                dve.add(lambda e, m=m: e.memset(m[0:DK, :, DV:DV1], 1.0 / DK), [token], sig["mem"])
                done["mem", live, t] = dve.add(
                    lambda e, m=m: e.memset(m[DK:P, :, 2 * DV1 - 1:2 * DV1], 1.0 / DK), (), sig["mem"])

        def read_memory(g, t):
            _, _, live = group_place(g)
            for j in range(2):
                bank = take_bank()
                ps = banks[bank][:, 0:2 * 2 * DV1].rearrange("p (c n) -> p c n", c=2)
                token = pe_job(bank, [matmul(ps[:, c], sq_t[:, 2 * j + c, t * P:(t + 1) * P],
                                             mem[:, live * TG + t, 2 * j + c], True, True) for c in range(2)],
                               after(("sq", g, 0), ("sq", g, 1), ("mem", live, t)), sig["num"])
                heads = ps.rearrange("p c (e n) -> p (c e) n", e=2)
                hs = slice(4 * j, 4 * j + 4)
                td = dve.add(lambda e, o=inv_den[:, t, hs], i=heads[:, :, DV]: e.reciprocal(o, i),
                             [token], sig["den"])
                tm = dve.add(tt(att_mem[:, t, hs], heads[:, :, 0:DV],
                                inv_den[:, t, hs].unsqueeze(2).to_broadcast([P, 4, DV]), ALU.mult),
                             [td, *after(("aturn", g - 1, t))], sig["mix_dve"])
                bank_free[bank] = [tm]
            done["num", g, t] = token
            done["att_mem", g, t] = tm

        def invert_sums(g, t, level):
            if level == 0:
                done["invsum", g, t] = dve.add(lambda e: e.reciprocal(inv_sum[:, t], row_sum[:, t]),
                                               after(("pexp", g, t, 1)), sig["den"])
            else:
                done["mix", g, t] = dve.add(ts(dot_scale[:, t], inv_sum[:, t], gcol(g, G_V11), None, ALU.mult),
                                            after(("invsum", g, t), ("scal", g)), sig["den"])

        def attend(g, t):
            bank = take_bank()
            ps = banks[bank][:].rearrange("p (h v) -> p h v", h=H)
            calls = []
            for h in range(H):
                cols = slice(h * DV, (h + 1) * DV)
                terms = ((pt_hi, v_hi), (pt_hi, v_lo), (pt_lo, v_hi))
                calls += [matmul(ps[:, h], a[:, t, h], b[:, t, cols], m == 0, m == 2)
                          for m, (a, b) in enumerate(terms)]
            token = pe_job(bank, calls, after(("pt", g, t, 0), ("pt", g, t, 1), ("v", g, t)), sig["pv"])
            done["pv", g, t] = token
            ti = done["mix", g, t]
            tm = dve.add(tt(att_dot[:, t], ps, dot_scale[:, t].unsqueeze(2).to_broadcast([P, H, DV]), ALU.mult),
                         [token, ti, *after(("mixed", g - 1, t))], sig["mix_dve"])
            bank_free[bank] = [tm]
            a = att_mem[:, t].rearrange("p h v -> p (h v)")
            b = att_dot[:, t].rearrange("p h v -> p (h v)")
            t1 = pool.add(tt(a, a, gate_in[:], ALU.mult), after(("att_mem", g, t), "gates"), sig["mix_pool"])
            t2 = pool.add(tt(b, b, gate_out[:], ALU.mult), [tm], sig["mix_pool"])
            done["mixed", g, t] = pool.add(tt(a, a, b, ALU.add), [t1, t2], sig["mix_pool"])

        def update_memory(g, t):
            _, _, live = group_place(g)
            for j in range(2):
                bank = take_bank()
                ps = banks[bank][:, 0:2 * 2 * DV1].rearrange("p (c n) -> p c n", c=2)
                vv = v1[:, t].rearrange("p (c e) n -> p c (e n)", e=2)
                token = pe_job(bank, [matmul(ps[:, c], sk[:, t, (2 * j + c) * P:(2 * j + c + 1) * P],
                                             vv[:, 2 * j + c], True, True) for c in range(2)],
                               after(("skrow", g, t), ("v1", g, t)), sig["upd"])
                for rs, cs in ((slice(0, DK), slice(0, DV1)), (slice(DK, P), slice(DV1, 2 * DV1))):
                    m = mem[rs, live * TG + t, 2 * j:2 * j + 2, cs]
                    tm = dve.add(tt(m, ps[rs, :, cs], m, ALU.add), [token, *after(("mem", live, t))], sig["mem"])
                bank_free[bank] = [tm]
            done["upd", g, t] = token
            done["mem", live, t] = tm

        def turn_att(g, t):
            bank = take_bank()
            ps = banks[bank][:].rearrange("p (k c) -> p k c", k=KT)
            a = att_mem[:, t].rearrange("p h v -> p (h v)")
            token = pe_job(bank, [transpose(ps[:, k], a[:, k * P:(k + 1) * P], ident32[:]) for k in range(KT)],
                           after(("mixed", g, t)), sig["aturn"])
            done["aturn", g, t] = token
            split(bank, at_hi[:, t], at_lo[:, t], ps, gcol(g, G_ASCALE), [token, *after(("outscal", g), ("wo", g - 1, t))],
                  ("at", g, t), sig["at_hi"], sig["at_lo"])

        def layer_stats(g, t, which, waits):
            r = rows[:, g % NX, t]
            ta = dve.add(lambda e: e.bn_stats(stats[:, which, t], r), waits, sig["stat"])
            ta = dve.add(lambda e: e.bn_aggr(mean_var[:, which, t], stats[:, which, t]), [ta], sig["stat"])
            tb = pool.add(lambda e: e.tensor_scalar(var_eps[:, which, t:t + 1], mean_var[:, which, t, 1:2],
                                                    EPS, None, ALU.add), [ta], sig["pow_in"])
            done["rstd", g, t, which] = pool.add(
                tt(rstd[:, which, t:t + 1], var_eps[:, which, t:t + 1], minus_half[:], ALU.pow),
                [tb, t_half], sig["rstd"])

        def normalise(g, t, which):
            r = rows[:, g % NX, t]
            done["norm", g, t, which] = dve.add(
                ts(r, r, mean_var[:, which, t, 0:1], rstd[:, which, t:t + 1], ALU.subtract, ALU.mult),
                after(("rstd", g, t, which)), sig["norm"])

        def project_out(g, t):
            bank = take_bank()
            terms = [(xs[:, t, k], wt["o"][:, k, :]) for k in range(KT)
                     for xs, wt in ((at_hi, w_hi), (at_hi, w_lo), (at_lo, w_hi))]
            token = pe_job(bank, [matmul(banks[bank][:], a, b, i == 0, i == len(terms) - 1)
                                  for i, (a, b) in enumerate(terms)],
                           after(("at", g, t), ("wsplit_lo", "o")), sig["wo"])
            done["wo", g, t] = token
            r = rows[:, g % NX, t]
            tr = dve.add(stt(r, banks[bank][:], gcol(g, G_WO), r, ALU.mult, ALU.add), [token], sig["resid"])
            bank_free[bank] = [tr]
            layer_stats(g, t, 0, [tr])

        def turn_y(g, t):
            bank = take_bank()
            ps = banks[bank][:].rearrange("p (k c) -> p k c", k=KT)
            r = rows[:, g % NX, t]
            token = pe_job(bank, [transpose(ps[:, k], r[:, k * P:(k + 1) * P], ident32[:]) for k in range(KT)],
                           after(("norm", g, t, 0)), sig["yturn"])
            toks = slice(t * P, (t + 1) * P)
            split(bank, yt_hi[:, g % 2, :, toks], yt_lo[:, g % 2, :, toks], ps, 2.0 ** 9,
                  [token, *after(("ffn1", g - 2, 7)), *([done["wturn", 31]] if g == 1 else [])], ("yt", g, t), sig["yt_hi"], sig["yt_lo"])
            done["yb", g, t] = pool.add(tt(r, r, b2_all[:], ALU.add), [token, t_small], sig["yb"])

        POOL_J = 1

        def ffn_up(g, j):
            bank = take_bank()
            ps = banks[bank][:].rearrange("p (c t) -> p c t", c=2)
            calls = []
            for c in range(2):
                cols = slice((2 * j + c) * P, (2 * j + c + 1) * P)
                terms = [(w1t[:, k, cols], ys[:, g % 2, k, :]) for k in range(KT) for ys in (yt_hi, yt_lo)]
                calls += [matmul(ps[:, c], a, b, i == 0, i == len(terms) - 1) for i, (a, b) in enumerate(terms)]
            token = pe_job(bank, calls, after(("yt", g, 0), ("yt", g, 1), ("wput", 1)), sig["ffn1"])
            done["ffn1", g, j] = token
            n = g * 8 + j
            buf = n % NH32
            for c in range(2):
                f = 2 * j + c
                tr = act.add(actv(h32[:, buf, c * GT:(c + 1) * GT], ps[:, c], ACT.Relu, scale=w(H_SCALE_Y),
                                  bias=b1_scaled[:, f:f + 1]),
                             [token, *after("hscale", ("h_lo", n - NH32), ("quant", 2, 3))], sig["relu"])
            bank_free[bank] = [tr]
            hi = h_hi[:, 2 * j:2 * j + 2].rearrange("p f t -> p (f t)")
            lo = h_lo[:, 2 * j:2 * j + 2].rearrange("p f t -> p (f t)")
            th = dve.add(lambda e: e.tensor_copy(hi, h32[:, buf]), [tr, *after(("ffn2", g - 1, 1))], sig["h_hi"])
            q, s = (pool, sig["h_lo_pool"]) if j % 2 == POOL_J else (dve, sig["h_lo"])
            done["h_lo", n] = done["h", g, j] = q.add(tt(lo, h32[:, buf], hi, ALU.subtract),
                                                      [th, *after(("ffn2", g - 1, 1))], s)

        PIECES = 4

        def ffn_down(g, t, piece):
            own = RING + t
            toks = slice(t * P, (t + 1) * P)
            fs = range(piece * FT // PIECES, (piece + 1) * FT // PIECES)
            terms = [(hs[:, f, toks], w2t[:, f, :], f, hs is h_lo) for f in fs for hs in (h_hi, h_lo)]
            calls = [matmul(banks[own][:], a, b, f == 0 and not is_lo, f == FT - 1 and is_lo)
                     for a, b, f, is_lo in terms]
            last = piece == PIECES - 1
            waits = after(*[("h", g, f // 2) for f in fs], ("wput", 2)) + (bank_free[own] if piece == 0 else [])
            for i, call in enumerate(calls):
                token = pe.add(call, waits if i == 0 else (), sig["ffn2"] if last and i == len(calls) - 1 else None)
            if not last:
                return
            done["ffn2", g, t] = token
            r = rows[:, g % NX, t]
            tr = dve.add(stt(r, banks[own][:], w(H_INV), r, ALU.mult, ALU.add),
                         [token, *after(("yb", g, t), "hscale")], sig["resid"])
            bank_free[own] = [tr]
            layer_stats(g, t, 1, [tr])

        def put_out(g, t):
            b0, seg, _ = group_place(g)
            done["out", g, t] = sp.add(
                lambda e: e.dma_start(out[b0 + t, seg * P:(seg + 1) * P, :], rows[:, g % NX, t]),
                after(("norm", g, t, 1)), s_xout[g % NX][t], 16)

        QK, V, SC, T4 = 24 * 109, 12 * 216, 8 * 56, 4 * 109
        MEM, PV = 4 * 222, 24 * 34

        def attention_steps(g):
            now, before, ahead = g < NG, 1 <= g <= NG, g + 1 < NG
            table = {}

            def step(name, when, cost, f, *args):
                table[name] = (when, cost, lambda: f(*args))

            for n in "kq":
                for j in range(2):
                    step(f"{n}{j}", now and g, QK, project_qk, g, n, j)
            for t in range(TG):
                step(f"v{t}", now, V, project_v, g, t)
                for half in range(2):
                    step(f"score{t}{half}", now, SC, scores, g, t, half)
                    step(f"turn_p{t}{half}", now, T4, turn_p, g, t, half)
                step(f"turn_sk{t}", now, T4, turn_sk, g, t)
                for level in range(2):
                    step(f"sums{t}{level}", now, 0, invert_sums, g, t, level)
                step(f"read{t}", now, MEM, read_memory, g, t)
                step(f"turn_x{t}", ahead, T4, turn_x, g + 1, t)
            for t, last, when in ((0, g, now), (1, g - 1, before)):
                step(f"attend{t}", when, PV, attend, last, t)
                step(f"update{t}", when, MEM, update_memory, last, t)
                step(f"turn_att{t}", when, T4, turn_att, last, t)
                step(f"out{t}", when, V, project_out, last, t)
                step(f"norm{t}", when, 0, normalise, last, t, 0)
                step(f"turn_y{t}", before, T4, turn_y, g - 1, t)
            step("max", ahead, 0, group_max, g + 1)
            for level in range(4):
                step(f"xscale{level}", ahead, 0, group_x_scale, g + 1, level)
            for level in range(3):
                step(f"scalars{level}", ahead, 0, group_scalars, g + 1, level)
            step("norm_end", g >= 2, 0, normalise, g - 2, 1, 1)
            step("put_end", g >= 2, 0, put_out, g - 2, 1)
            step("load", 1 <= g and g + 2 < NG, 0, load_x, g + 2)
            names = [half.split() for half in TURN]
            assert sorted(names[0] + names[1]) == sorted(table)
            return [[table[n][1:] for n in half if table[n][0]] for half in names]

        def ffn_steps(g):
            if not 0 <= g < NG:
                return [], []
            steps = [(16 * 109, lambda j=j: ffn_up(g, j)) for j in range(FT // 2)]
            for t in range(TG):
                for piece in range(PIECES):
                    steps.append((8 * 216, lambda t=t, p=piece: ffn_down(g, t, p)))
                    if t == 1 and piece == 0:
                        steps.append((0, lambda: normalise(g, 0, 1)))
                        steps.append((0, lambda: put_out(g, 0)))
            return steps[:EARLY], steps[EARLY:]

        def merged(a, b):
            total_a, total_b = sum(c for c, _ in a) or 1, sum(c for c, _ in b) or 1
            at_a = at_b = 0
            a, b = list(a), list(b)
            while a or b:
                if not b or (a and at_a / total_a <= at_b / total_b):
                    cost, f = a.pop(0)
                    at_a += cost
                else:
                    cost, f = b.pop(0)
                    at_b += cost
                f()

        group_max(0)
        for level in range(4):
            group_x_scale(0, level)
        scale_w("k")
        turn_x(0, 0)
        turn_x(0, 1)
        split_w("k")
        scale_w("q")
        scale_w("v")
        for level in range(2):
            group_scalars(0, level)
        project_qk(0, "k", 0)
        split_w("q")
        project_qk(0, "k", 1)
        project_qk(0, "q", 0)
        split_w("v")
        project_qk(0, "q", 1)
        scale_w("o")
        split_w("o")
        group_scalars(0, 2)
        load_x(1)
        for i in range(4):
            load_ffn_w(1, i)
        load_x(2)
        for live in range(LIVE):
            reset_memory(live)

        SUM_PACE = 2000

        def prepare_ffn_w(m):
            steps = [(SUM_PACE, lambda i=i: sum_ffn_w(m, i)) for i in range(4)]
            steps.append((500, lambda: threshold(m)))
            blocks = [(m, i, b) for i in range(4) for b in range(4)]
            for n in range(len(blocks) + 1):
                if n < len(blocks):
                    steps.append((0, lambda a=blocks[n]: compare(*a)))
                    if m == 1 and blocks[n][2] == 3:
                        steps.append((0, lambda i=blocks[n][1]: load_ffn_w(2, i)))
                if n:
                    steps.append((500, lambda a=blocks[n - 1]: turn_w(*a)))
            return steps

        first, second = attention_steps(0)
        prep = prepare_ffn_w(1)
        prep[9:9] = [(0, prepare_gates), (0, prepare_ffn_scale)]
        merged(first + second, prep)

        for g in range(1, NG + 2):
            if g < NG and g % (LIVE * NSEG) < LIVE and g >= LIVE * NSEG:
                reset_memory(group_place(g)[2])
            first, second = attention_steps(g)
            merged(first, ffn_steps(g - 2)[1] if g > 1 else prepare_ffn_w(2))
            merged(second, ffn_steps(g - 1)[0])

        sp.add(None, [(s.sem, s.count) for pair in s_xout for s in pair])

        block = ctx.enter_context(nc.Block())

        @block.sync
        def _(eng):
            sp.replay(eng)

        @block.tensor
        def _(eng):
            pe.replay(eng)

        @block.vector
        def _(eng):
            dve.replay(eng)

        @block.scalar
        def _(eng):
            act.replay(eng)

        @block.gpsimd
        def _(eng):
            pool.replay(eng)


_INS = ["L0_attn_x", "L0_attn_Wq", "L0_attn_Wk", "L0_attn_Wv", "L0_attn_betas", "L0_attn_Wo",
        "L0_ffn_W1", "L0_ffn_b1", "L0_ffn_W2", "L0_ffn_b2"]


def kernel(**inputs):
    import numpy as np
    import concourse.bacc as bacc
    from concourse.bass_utils import run_bass_kernel_spmd

    nc = bacc.Bacc("TRN2", target_bir_lowering=False, num_devices=1)
    arrays, args = {}, []
    for name in _INS:
        a = np.ascontiguousarray(inputs[name])
        arrays[f"in_{name}"] = a
        args.append(nc.dram_tensor(f"in_{name}", a.shape, mybir.dt.from_np(a.dtype), kind="ExternalInput").ap())
    shape = inputs["L0_attn_x"].shape
    args.append(nc.dram_tensor("out_rows", shape, F32, kind="ExternalOutput").ap())
    build_program(nc, *args)
    result = run_bass_kernel_spmd(nc, [arrays], core_ids=[0])
    return result.results[0]["out_rows"]
```

```python
from contextlib import ExitStack

import concourse.bass as bass
import concourse.mybir as mybir

ALU = mybir.AluOpType
ACT = mybir.ActivationFunctionType
F32 = mybir.dt.float32
F16 = mybir.dt.float16
U32 = mybir.dt.uint32
AX_X = mybir.AxisListType.X
AX_XY = mybir.AxisListType.XY
RMAX = bass.bass_isa.ReduceOp.max
RADD = bass.bass_isa.ReduceOp.add

P = 128
RING = 6
EXPONENT = 0x7F800000
EPS = 1e-5


TURN = (
    "update1 max k0 turn_y0 q0 attend1 k1 turn_att1 xscale0 q1 v0 score00 out1 score11 "
    "score10 xscale1 norm1 xscale2 score01 turn_y1 v1 sums00 turn_p00 turn_sk0",
    "turn_p01 norm_end turn_sk1 xscale3 put_end load sums01 scalars0 read0 attend0 scalars1 "
    "read1 turn_p10 sums10 turn_p11 turn_x0 update0 sums11 scalars2 turn_att0 turn_x1 out0 "
    "norm0",
)

START = """
    first_max first_xscale0 first_xscale1 first_xscale2 max_k first_xscale3 scale_k split_k1
    split_k0 first_turn_x0 first_turn_x1 max_v scale_v max_q scale_q first_scalars0
    first_scalars1 split_q0 split_v1 split_q1 k0 split_v0 k1 max load13 q1 load20 max_o sum11
    scale_o q0 sum13 split_o0 load12 sum10 sum12 first_scalars2 score01 score11 xscale0
    threshold1 v0 gates split_o1 turn_p11 load21 turn_sk0 turn_p01 xscale1 v1 score00 xscale2
    sums00 ffn_scale read0 turn_p00 sum20 sum22 turn_sk1 xscale3 block score10 block block sum23
    block sums01 scalars0 attend0 scalars1 block read1 turn_p10 block sums10 block block
    turn_att0 sums11 block update0 block turn_x0 block block block sum21 threshold2 block out0
    block block turn_x1 block block block block block block scalars2 block block block norm0
"""

EARLY = 6


class Signal:

    def __init__(self, sem):
        self.sem = sem
        self.count = 0


class Queue:

    def __init__(self):
        self.items = []
        self.waited = {}

    def add(self, emit, after=(), signal=None, by=1):
        waits = []
        for token in after:
            if token is None:
                continue
            sem, value = token
            if self.waited.get(id(sem), 0) < value:
                self.waited[id(sem)] = value
                waits.append(token)
        if signal is not None:
            signal.count += by
        self.items.append((waits, emit, signal.sem if signal else None, by))
        return (signal.sem, signal.count) if signal else None

    def replay(self, eng):
        for waits, emit, sem, by in self.items:
            for s, value in waits:
                eng.wait_ge(s, value)
            ins = emit(eng) if emit else None
            if sem is not None:
                ins.then_inc(sem, by)


def build_program(nc, x, Wq, Wk, Wv, betas, Wo, W1, b1, W2, b2, out):
    B, S, D = x.shape
    H, DV = betas.shape[1], betas.shape[3]
    DK = Wq.shape[1] // H
    F = W1.shape[0]
    KT = D // P
    FT = F // P
    NPAIR = H * DK // P
    NSEG = S // P
    TG = 2
    GT = TG * P
    LIVE = 2
    NG = B // TG * NSEG
    DV1 = DV + 1
    assert DK == DV == 64 and D == 512 and H == 8 and B % (TG * LIVE) == 0 and S % P == 0

    ctx = ExitStack()
    with ctx:
        def sb(name, shape, dt=F32):
            return ctx.enter_context(nc.sbuf_tensor(name, shape, dt))

        def signal(name):
            return Signal(ctx.enter_context(nc.semaphore(name)))

        banks = [ctx.enter_context(nc.psum_tensor(f"bank{i}", [P, 512], F32)) for i in range(8)]

        w_hi = {n: sb(f"w{n}_hi", [P, KT, D], F16) for n in "kqvo"}
        w_lo = {n: sb(f"w{n}_lo", [P, KT, D], F16) for n in "kqvo"}
        w1t = sb("w1t", [P, KT, F], F16)
        w2t = sb("w2t", [P, FT, D], F16)
        arena = sb("arena", [P, 4, 2048], F32)
        ident32 = sb("ident32", [P, P])
        ident16 = sb("ident16", [P, P], F16)
        minus16 = sb("minus16", [P, P], F16)
        gate_in = sb("gate_in", [P, D])
        gate_out = sb("gate_out", [P, D])
        b2_all = sb("b2_all", [P, D])
        b1_col = sb("b1_col", [P, FT])
        b1_rows = sb("b1_rows", [FT, P])
        b1_scaled = sb("b1_scaled", [P, FT])
        minus_half = sb("minus_half", [P, 1])
        ws = sb("wscalars", [P, 40])
        gs = sb("gscalars", [P, NG, 16])

        NX = 4
        rows = sb("rows", [P, NX, TG, D])
        xt_hi = sb("xt_hi", [P, KT, GT], F16)
        xt_lo = sb("xt_lo", [P, KT, GT], F16)
        q_both = sb("q_both", [P, NPAIR, 2, GT], F16)
        k_hi = sb("k_hi", [P, NPAIR, 2, GT], F16)
        k_lo = sb("k_lo", [P, NPAIR, 2, GT], F16)
        sq_t = sb("sq_t", [P, NPAIR, GT])
        sk_t = sb("sk_t", [P, NPAIR, GT])
        exp_tmp = sb("exp_tmp", [P, 512])
        relu_tmp = sb("relu_tmp", [P, 512])
        v_hi = sb("v_hi", [P, TG, D], F16)
        v_lo = sb("v_lo", [P, TG, D], F16)
        v1 = sb("v1", [P, TG, H, DV1])
        sk = sb("sk", [P, TG, H * DK])
        prob = sb("prob", [P, TG, H, P])
        pt_hi = sb("pt_hi", [P, TG, H, P], F16)
        pt_lo = sb("pt_lo", [P, TG, H, P], F16)
        att_mem = sb("att_mem", [P, TG, H, DV])
        att_dot = sb("att_dot", [P, TG, H, DV])
        at_hi = sb("at_hi", [P, TG, KT, P], F16)
        at_lo = sb("at_lo", [P, TG, KT, P], F16)
        mem = sb("mem", [P, LIVE * TG, NPAIR, 2 * DV1])
        row_max = sb("row_max", [P, TG, H])
        exp_bias = sb("exp_bias", [P, TG, H])
        row_sum = sb("row_sum", [P, TG, H])
        inv_sum = sb("inv_sum", [P, TG, H])
        dot_scale = sb("dot_scale", [P, TG, H])
        inv_den = sb("inv_den", [P, TG, H])
        amax = sb("amax", [P, 2])
        stats = sb("stats", [P, 2, TG, 6])
        mean_var = sb("mean_var", [P, 2, TG, 2])
        var_eps = sb("var_eps", [P, 2, TG])
        rstd = sb("rstd", [P, 2, TG])

        flat = arena[:].rearrange("p a b -> p (a b)")
        h_hi = flat[:, 0:2048].bitcast(F16).rearrange("p (f t) -> p f t", f=FT)
        h_lo = flat[:, 2048:4096].bitcast(F16).rearrange("p (f t) -> p f t", f=FT)
        NH32 = 4
        h32 = flat[:, 4096:4096 + NH32 * 512].rearrange("p (b t) -> p b t", b=NH32)
        yt_hi = sb("yt_hi", [P, 2, KT, GT], F16)
        yt_lo = sb("yt_lo", [P, 2, KT, GT], F16)
        wabove = yt_hi[:, 1].rearrange("p k t -> p (k t)").rearrange("p (b n) -> p b n", b=2)
        wbelow = yt_lo[:, 1].rearrange("p k t -> p (k t)").rearrange("p (b n) -> p b n", b=2)

        names = ("consts gp_work bload "
                 "wmax wsum scal wsplit_hi wsplit_lo above below below_pool wturn wput amax_all "
                 "xturn xt_hi xt_lo kproj qproj vproj kq_hi kq_lo kq_exp kq_sk v_hi v_lo v1 "
                 "score smax pexp pturn pt_hi pt_lo pv num skturn sk upd mem den mix_dve mix_pool "
                 "aturn at_hi at_lo wo resid stat pow_in rstd norm yturn yt_hi yt_lo yb "
                 "ffn1 relu h_hi h_lo h_lo_pool ffn2 chain actmisc")
        sig = {n: signal("s_" + n) for n in names.split()}

        s_wload = [signal(f"s_wload{i}") for i in range(8)]
        s_xload = [signal(f"s_xload{i}") for i in range(NX)]
        s_xout = [[signal(f"s_xout{i}_{t}") for t in range(TG)] for i in range(NX)]

        pe, act, dve, pool, sp = (Queue() for _ in range(5))
        done = {}

        def after(*keys):
            return [done.get(k) for k in keys]

        bank_free = [[] for _ in range(8)]
        ring_at = [0]

        def take_bank():
            b = ring_at[0] % RING
            ring_at[0] += 1
            return b

        def transpose(dst, src, ident):
            return lambda e: e.transpose(dst, src, ident)

        def matmul(dst, lhsT, rhs, start, stop):
            return lambda e: e.matmul(dst, lhsT, rhs, start=start, stop=stop)

        def pe_job(bank, calls, waits, s):
            waits = list(waits) + bank_free[bank]
            for n, call in enumerate(calls):
                token = pe.add(call, waits if n == 0 else (), s if n == len(calls) - 1 else None)
            bank_free[bank] = []
            return token

        def chain(calls, first=()):
            token = None
            for call in calls:
                token = dve.add(call, [*first, token], sig["chain"])
                first = ()
            return token

        def ts(o, i, s1, s2, op0, op1=None):
            if op1 is None:
                return lambda e: e.tensor_scalar(o, i, s1, None, op0)
            return lambda e: e.tensor_scalar(o, i, s1, s2, op0, op1)

        def stt(o, i0, s, i1, op0, op1):
            return lambda e: e.scalar_tensor_tensor(out=o, in0=i0, scalar=s, in1=i1, op0=op0, op1=op1)

        def tt(o, a, b, op):
            return lambda e: e.tensor_tensor(o, a, b, op)

        def actv(o, i, f, **kw):
            return lambda e: e.activation(o, i, f, **kw)

        def round_down(o, i):
            return lambda e: e.tensor_scalar(o.bitcast(U32), i.bitcast(U32), EXPONENT, None, ALU.bitwise_and)

        def w(i):
            return ws[:, i:i + 1]

        INV_W = {"k": 0, "q": 1, "v": 2, "o": 3}
        SCALE_W = {"k": 4, "q": 5, "v": 6, "o": 7}
        WMAX = {"k": 8, "q": 9, "v": 10, "o": 11}
        WALL = {"k": 12, "q": 13, "v": 14, "o": 15}
        SUM_PART = {1: 16, 2: 20}
        SUM_ROW, SUM_ALL = {1: 24, 2: 25}, {1: 26, 2: 27}
        ABOVE, BELOW = {1: 28, 2: 29}, {1: 30, 2: 31}
        H_INV, H_SCALE, H_SCALE_Y = 32, 33, 34
        B1_MAX, B1_ALL = 35, 36

        C = sig["consts"]
        z = pool.add(lambda e: e.memset(ident32[:], 0.0), (), C)
        t_ident = pool.add(lambda e: e.affine_select(
            out=ident32[:], in_=ident32[:], compare_op=ALU.not_equal, fill=1.0, base=0,
            pattern=[[-1, P]], channel_multiplier=1), [z], C)
        t_half = pool.add(lambda e: e.memset(minus_half[:], -0.5), (), C)
        pool.add(lambda e: e.memset(k_lo[:].rearrange("p a b t -> p (a b t)").bitcast(U32), 0), (), C)
        t_zero = pool.add(lambda e: e.memset(v1[:, :, :, DV:DV1], 1.0), (), C)
        dve.add(lambda e: e.tensor_copy(ident16[:], ident32[:]), [t_ident], sig["chain"])
        t_ident16 = dve.add(ts(minus16[:], ident32[:], -1.0, None, ALU.mult), (), sig["chain"])

        raw = {n: arena[:, i, :].rearrange("p (k n) -> p k n", k=KT) for i, n in enumerate("kqvo")}
        dram_w = {"k": Wk, "q": Wq, "v": Wv, "o": Wo}

        def group_place(g):
            half, r = divmod(g, LIVE * NSEG)
            seg, live = divmod(r, LIVE)
            return half * LIVE * TG + live * TG, seg, live

        def ffn_raw(m, i):
            if m == 1 and i < 2:
                return w2t[:, 8 * i:8 * i + 8].rearrange("p f n -> p (f n)").bitcast(F32)
            return arena[:, (i + 2) % 4, :]

        def for_sum(i):
            return w1t[:, :, (i - 2) * F // 2:(i - 1) * F // 2].bitcast(F32)

        def load_for_sum(i):
            src = W2.rearrange("(i p) (k f) -> i p k f", p=P, k=KT)[i]
            done["for_sum", i] = sp.add(lambda e: e.dma_start(for_sum(i), src), (), s_wload[4 + i], 16)

        def load_x(g):
            b0, seg, _ = group_place(g)
            src = x[b0:b0 + TG, seg * P:(seg + 1) * P, :].rearrange("b p d -> p b d")
            done["x", g] = sp.add(lambda e: e.dma_start(rows[:, g % NX], src),
                                  after(("out", g - NX, 0), ("out", g - NX, 1),
                                        *(["unread"] if g == NX - 1 else [])), s_xload[g % NX], 16)

        def load_w(n):
            src = dram_w[n].rearrange("(k p) n -> p k n", p=P)
            done["raw", n] = sp.add(lambda e: e.dma_start(raw[n], src), (), s_wload["kqvo".index(n)], 16)

        def load_ffn_w(m, i):
            if m == 1:
                src = W1.rearrange("(i f p) d -> i p f d", i=4, p=P)[i]
                dst = ffn_raw(m, i).rearrange("p (f d) -> p f d", d=D)
            else:
                src = W2.rearrange("(i p) f -> i p f", p=P)[i]
                dst = ffn_raw(m, i)
            before = {(1, 2): "k", (1, 3): "q", (2, 0): "v", (2, 1): "o"}.get((m, i))
            waits = [done["wsplit", before, j] for j in range(2)] if before else []
            if m == 2 and i >= 2:
                waits = [done["above", 1, i, 3], done["below", 1, i, 3]]
            buf = 4 + i if m == 1 and i < 2 else (i + 2) % 4
            done["raw", m, i] = sp.add(lambda e: e.dma_start(dst, src), waits, s_wload[buf], 16)

        load_x(0)
        for n in "kqv":
            load_w(n)
        sp.add(lambda e: e.dma_start(gate_in[:], betas.rearrange("a h b v -> (a b) (h v)")
                                          .rearrange("a n -> (a n)").partition_broadcast(P)),
                    (), sig["bload"], 16)
        sp.add(lambda e: e.dma_start(b2_all[:], b2.partition_broadcast(P)), (), sig["bload"], 16)
        sp.add(lambda e: e.dma_start(b1_rows[:], b1.rearrange("(f p) -> f p", p=P)), (), sig["bload"], 16)
        t_small = (sig["bload"].sem, sig["bload"].count)
        for i in range(2):
            load_ffn_w(1, i)
        load_w("o")
        for i in (2, 3):
            load_for_sum(i)

        def max_w(n):
            t = dve.add(lambda e: e.tensor_reduce(w(WMAX[n]), raw[n], AX_XY, ALU.max,
                                                  apply_absolute_value=True),
                        after(("raw", n)), sig["wmax"])
            done["wmax", n] = pool.add(
                lambda e: e.partition_all_reduce(w(WALL[n]), w(WMAX[n]), P, RMAX), [t], sig["gp_work"])

        def scale_w(n):
            done["wscale", n] = chain(
                [ts(w(WALL[n]), w(WALL[n]), 2.0 ** -60, None, ALU.max),
                 round_down(w(INV_W[n]), w(WALL[n])),
                 ts(w(INV_W[n]), w(INV_W[n]), 2.0 ** -14, None, ALU.mult),
                 lambda e: e.reciprocal(w(SCALE_W[n]), w(INV_W[n]))], after(("wmax", n)))

        def split_w(n, j):
            t = done["wscale", n]
            hi, lo, full = (a[:, :, j * D // 2:(j + 1) * D // 2] for a in (w_hi[n], w_lo[n], raw[n]))
            t_hi = act.add(actv(hi, full, ACT.Copy, scale=w(SCALE_W[n])), [t], sig["wsplit_hi"])
            done["wsplit", n, j] = dve.add(stt(lo, full, w(SCALE_W[n]), hi, ALU.mult, ALU.subtract),
                                           [t_hi, t], sig["wsplit_lo"])

        NBLOCKS = 2 * 16
        unread = rows[:, NX - 1].rearrange("p t d -> p (t d)").bitcast(mybir.dt.bfloat16)

        def sum_ffn_w(m, i):
            src, loaded = ffn_raw(m, i), ("raw", m, i)
            dst = unread
            if m == 2 and i >= 2:
                src, loaded = for_sum(i), ("for_sum", i)
                dst = unread.rearrange("p (k f) -> p k f", k=KT)
            done["wsum", m, i] = act.add(
                actv(dst, src, ACT.Abs, accum_out=w(SUM_PART[m] + i)),
                [done[loaded], *after("unread")], sig["wsum"])
            done["unread"] = done["wsum", m, i]

        def threshold(m):
            t = dve.add(lambda e: e.tensor_reduce(w(SUM_ROW[m]), ws[:, SUM_PART[m]:SUM_PART[m] + 4],
                                                  AX_X, ALU.add),
                        [done["wsum", m, i] for i in range(4)], sig["wmax"])
            t = pool.add(lambda e: e.partition_all_reduce(w(SUM_ALL[m]), w(SUM_ROW[m]), P, RADD), [t], sig["gp_work"])
            done["threshold", m] = chain(
                [ts(w(SUM_ALL[m]), w(SUM_ALL[m]), 1.0 / (F * D), EPS, ALU.mult, ALU.add),
                 ts(w(ABOVE[m]), w(SUM_ALL[m]), 0.5, None, ALU.mult),
                 ts(w(BELOW[m]), w(SUM_ALL[m]), -0.5, None, ALU.mult)], [t])

        def compare(m, i, b):
            n = ((m - 1) * 4 + i) * 4 + b
            src = ffn_raw(m, i)[:, b * 512:(b + 1) * 512]
            waits = [done["threshold", m], done["raw", m, i], *after(("wturn", n - 2))]
            done["above", m, i, b] = dve.add(ts(wabove[:, n % 2, :], src, w(ABOVE[m]), None, ALU.is_gt),
                                             waits, sig["above"])
            q, s = (pool, sig["below_pool"]) if n % 2 else (dve, sig["below"])
            done["below", m, i, b] = q.add(ts(wbelow[:, n % 2, :], src, w(BELOW[m]), None, ALU.is_lt), waits, s)

        def turn_w(m, i, b):
            n = ((m - 1) * 4 + i) * 4 + b
            bank = take_bank()
            ps = banks[bank][:].rearrange("p (j c) -> p j c", j=4)
            calls = []
            for j in range(4):
                cols = slice(j * P, (j + 1) * P)
                calls += [matmul(ps[:, j], wabove[:, n % 2, cols], ident16[:], True, False),
                          matmul(ps[:, j], wbelow[:, n % 2, cols], minus16[:], False, True)]
            t = pe_job(bank, calls, [t_ident16, *after(("above", m, i, b), ("below", m, i, b))], sig["wturn"])
            done["wturn", n] = t
            f0 = (i * 4 + b) * P
            dst = w1t[:, :, f0:f0 + P] if m == 1 else w2t[:, b * 4:b * 4 + 4, i * P:(i + 1) * P]
            done["wput", m] = act.add(actv(dst, ps, ACT.Copy), [t, done["wsum", 2, 2 + i // 2]], sig["wput"])
            bank_free[bank] = [done["wput", m]]

        def prepare_ffn_scale():
            bank = take_bank()
            ps = banks[bank][:, 0:FT]
            t = pe_job(bank, [transpose(ps, b1_rows[:], ident32[0:FT, 0:FT])], [t_small, t_ident], sig["wturn"])
            t = dve.add(lambda e: e.tensor_copy(b1_col[:], ps), [t], sig["wmax"])
            bank_free[bank] = [t]
            t = dve.add(lambda e: e.tensor_reduce(w(B1_MAX), b1_col[:], AX_X, ALU.max, apply_absolute_value=True),
                        [t], sig["wmax"])
            t = pool.add(lambda e: e.partition_all_reduce(w(B1_ALL), w(B1_MAX), P, RMAX), [t], sig["gp_work"])
            done["hscale"] = chain(
                [ts(w(B1_ALL), w(B1_ALL), float(D), None, ALU.add),
                 round_down(w(H_INV), w(B1_ALL)),
                 ts(w(H_INV), w(H_INV), 2.0 ** -14, None, ALU.mult),
                 lambda e: e.reciprocal(w(H_SCALE), w(H_INV)),
                 ts(w(H_SCALE_Y), w(H_SCALE), 2.0 ** -9, None, ALU.mult),
                 ts(b1_scaled[:], b1_col[:], w(H_SCALE), None, ALU.mult)], [t])

        def prepare_gates():
            t = act.add(actv(gate_out[:], gate_in[:], ACT.Exp, scale=-1.0), [t_small], sig["actmisc"])
            done["gates"] = chain(
                [ts(gate_out[:], gate_out[:], 1.0, None, ALU.add),
                 lambda e: e.reciprocal(gate_in[:], gate_out[:]),
                 ts(gate_out[:], gate_in[:], -1.0, 1.0, ALU.mult, ALU.add)], [t])

        (G_ALL, G_POW, G_INV, G_SCALE, G_Q, G_K, G_V, G_EXP, G_V11, G_RUN, G_AINV, G_ASCALE, G_WO) = range(13)

        def gcol(g, i):
            return gs[:, g, i:i + 1]

        def group_max(g):
            t = dve.add(lambda e: e.tensor_reduce(amax[:, g % 2:g % 2 + 1], rows[:, g % NX], AX_XY, ALU.max,
                                                  apply_absolute_value=True),
                        after(("x", g)), sig["wmax"])
            done["amax_all", g] = pool.add(
                lambda e: e.partition_all_reduce(gcol(g, G_ALL), amax[:, g % 2:g % 2 + 1], P, RMAX),
                [t], sig["amax_all"])

        def side_by_side(calls, waits, key):
            for i, call in enumerate(calls):
                done[key] = dve.add(call, waits if i == 0 else (), sig["scal"])

        def group_x_scale(g, level):
            call, before = [
                (ts(gcol(g, G_ALL), gcol(g, G_ALL), 2.0 ** -60, None, ALU.max), ("amax_all", g)),
                (round_down(gcol(g, G_POW), gcol(g, G_ALL)), ("xclamp", g)),
                (ts(gcol(g, G_INV), gcol(g, G_POW), 2.0 ** -14, None, ALU.mult), ("xpow", g)),
                (lambda e: e.reciprocal(gcol(g, G_SCALE), gcol(g, G_INV)), ("xinv", g))][level]
            side_by_side([call], after(before), (("xclamp", "xpow", "xinv", "xscale")[level], g))

        def group_scalars(g, level):
            _, seg, _ = group_place(g)
            before = gcol(g - LIVE, G_POW if seg == 1 else G_RUN) if seg else gcol(g, G_POW)
            if level == 0:
                side_by_side(
                    [ts(gcol(g, G_Q), gcol(g, G_INV), w(INV_W["q"]), None, ALU.mult),
                     ts(gcol(g, G_K), gcol(g, G_INV), w(INV_W["k"]), None, ALU.mult),
                     ts(gcol(g, G_V), gcol(g, G_INV), w(INV_W["v"]), None, ALU.mult),
                     tt(gcol(g, G_RUN), gcol(g, G_POW), before, ALU.max)],
                    [done["xscale", g], *[done["wscale", n] for n in "kqv"]], ("scal0", g))
            elif level == 1:
                side_by_side(
                    [ts(gcol(g, G_EXP), gcol(g, G_Q), gcol(g, G_K), DK ** -0.5 * 2.0 ** 48, ALU.mult, ALU.mult),
                     ts(gcol(g, G_V11), gcol(g, G_V), 2.0 ** 11, None, ALU.mult),
                     ts(gcol(g, G_AINV), gcol(g, G_RUN), w(INV_W["v"]), 2.0 ** 11, ALU.mult, ALU.mult)],
                    [done["scal0", g]], ("scal", g))
            else:
                side_by_side(
                    [lambda e: e.reciprocal(gcol(g, G_ASCALE), gcol(g, G_AINV)),
                     ts(gcol(g, G_WO), gcol(g, G_AINV), w(INV_W["o"]), None, ALU.mult)],
                    [done["scal", g], done["wscale", "o"]], ("outscal", g))

        def split_hi(hi, src, scale, waits, s_hi):
            return act.add(actv(hi, src, ACT.Copy, scale=scale), waits, s_hi)

        def split_lo(hi, lo, src, scale, waits, s_lo):
            return dve.add(stt(lo, src, scale, hi, ALU.mult, ALU.subtract), waits, s_lo)

        def split(bank, hi, lo, src, scale, waits, key, s_hi, s_lo):
            t_hi = split_hi(hi, src, scale, waits, s_hi)
            done[key] = split_lo(hi, lo, src, scale, [t_hi, *waits], s_lo)
            bank_free[bank] += [done[key]]

        def turn_x(g, t):
            bank = take_bank()
            ps = banks[bank][:].rearrange("p (k c) -> p k c", k=KT)
            token = pe_job(bank, [transpose(ps[:, k], rows[:, g % NX, t, k * P:(k + 1) * P], ident32[:])
                                  for k in range(KT)], [t_ident, *after(("x", g))], sig["xturn"])
            split(bank, xt_hi[:, :, t * P:(t + 1) * P], xt_lo[:, :, t * P:(t + 1) * P], ps, gcol(g, G_SCALE),
                  [token, *after(("xscale", g), ("vproj", g - 1, 1))], ("xt", g, t), sig["xt_hi"], sig["xt_lo"])

        def project_qk(g, n, j):
            bank = take_bank()
            ps = banks[bank][:].rearrange("p (c t) -> p c t", c=2)
            calls = []
            for c in range(2):
                cols = slice((2 * j + c) * P, (2 * j + c + 1) * P)
                terms = [(wt[n][:, k, cols], xs[:, k, :]) for k in range(KT)
                         for wt, xs in ((w_hi, xt_hi), (w_hi, xt_lo), (w_lo, xt_hi))]
                calls += [matmul(ps[:, c], a, b, i == 0, i == len(terms) - 1) for i, (a, b) in enumerate(terms)]
            token = pe_job(bank, calls, after(("xt", g, 0), ("xt", g, 1)) + [done["wsplit", n, j]], sig[n + "proj"])
            pairs = slice(2 * j, 2 * j + 2)
            scored = after(("score", g - 1, 1, 1))
            halves = (slice(0, DK), slice(DK, P))
            for e, own in enumerate(halves):
                dst = q_both if n == "q" else k_hi
                split_hi(dst[own, pairs, e], ps[own], 2.0 ** -24, [token, t_zero, *scored], sig["kq_hi"])
            scale = gcol(g, G_Q if n == "q" else G_K)
            flat_ps = banks[bank][:]
            act.add(actv(exp_tmp[:], flat_ps, ACT.Exp, scale=scale), after(("scal", g), "elu"), sig["kq_exp"])
            t_r = act.add(actv(relu_tmp[:], flat_ps, ACT.Relu, scale=scale), (), sig["kq_exp"])
            for e, own in enumerate(halves):
                other = halves[1 - e]
                if n == "q":
                    t_lo = split_lo(q_both[own, pairs, e], q_both[other, pairs, e], ps[own], 2.0 ** -24,
                                    [t_r, *scored], sig["kq_lo"])
                else:
                    t_lo = split_lo(k_hi[own, pairs, e], k_lo[own, pairs, e], ps[own], 2.0 ** -24,
                                    [t_r, *scored], sig["kq_lo"])
            bank_free[bank] = [t_lo]
            done[n, g, j] = t_lo
            if n == "k":
                for e, own in enumerate(halves):
                    done[n, g, j] = dve.add(
                        lambda eng, e=e, a=own, b=halves[1 - e]: eng.tensor_copy(k_hi[b, pairs, e], k_hi[a, pairs, e]),
                        (), sig["kq_lo"])
            dst = (sq_t if n == "q" else sk_t)[:, pairs].rearrange("p c t -> p (c t)")
            waits = after(("num", g - 1, 1)) if n == "q" else after(("skturn", g - 1, 1))
            done["elu"] = done["s" + n, g, j] = dve.add(
                stt(dst, exp_tmp[:], 1.0, relu_tmp[:], ALU.min, ALU.add), [t_r, *waits], sig["kq_sk"])

        def project_v(g, t):
            bank = take_bank()
            toks = slice(t * P, (t + 1) * P)
            terms = [(xs[:, k, toks], wt["v"][:, k, :]) for k in range(KT)
                     for xs, wt in ((xt_hi, w_hi), (xt_hi, w_lo), (xt_lo, w_hi))]
            token = pe_job(bank, [matmul(banks[bank][:], a, b, i == 0, i == len(terms) - 1)
                                  for i, (a, b) in enumerate(terms)],
                           [done["xt", g, t], done["wsplit", "v", 0], done["wsplit", "v", 1]], sig["vproj"])
            done["vproj", g, t] = token
            read = after(("pv", g - 1, t))
            split_hi(v_hi[:, t], banks[bank][:], 2.0 ** -24, [token, *read], sig["v_hi"])
            done["v1", g, t] = act.add(
                actv(v1[:, t, :, 0:DV], banks[bank][:].rearrange("p (h v) -> p h v", h=H), ACT.Copy,
                     scale=gcol(g, G_V)), after(("scal", g), ("upd", g - 1, t)), sig["v1"])
            done["v", g, t] = split_lo(v_hi[:, t], v_lo[:, t], banks[bank][:], 2.0 ** -24,
                                       [done["v1", g, t], *read], sig["v_lo"])
            bank_free[bank] = [done["v", g, t]]

        def scores(g, t, half):
            bank = take_bank()
            ps = banks[bank][:].rearrange("p (h t) -> p h t", h=4)
            toks = slice(t * P, (t + 1) * P)
            calls = []
            for i in range(4):
                c, e = 2 * half + i // 2, i % 2
                calls += [matmul(ps[:, i], q_both[:, c, e, toks], k_hi[:, c, e, toks], True, False),
                          matmul(ps[:, i], q_both[:, c, e, toks], k_lo[:, c, e, toks], False, True)]
            token = pe_job(bank, calls, after(("q", g, half), ("k", g, half)), sig["score"])
            done["score", g, t, half] = token
            hs = slice(4 * half, 4 * half + 4)
            tm = dve.add(lambda e: e.tensor_reduce(row_max[:, t, hs], ps, AX_X, ALU.max),
                         [token], sig["smax"])
            tm = dve.add(ts(exp_bias[:, t, hs], row_max[:, t, hs], gcol(g, G_EXP), -1.0, ALU.mult, ALU.mult),
                         [tm, *after(("scal", g), ("pexp", g - 1, t, half))], sig["smax"])
            for i in range(4):
                h = 4 * half + i
                te = act.add(actv(prob[:, t, h], ps[:, i], ACT.Exp, scale=gcol(g, G_EXP),
                                  bias=exp_bias[:, t, h:h + 1], accum_out=row_sum[:, t, h:h + 1]),
                             [tm, *after(("pturn", g - 1, t, half), ("mix", g - 1, t))], sig["pexp"])
            done["pexp", g, t, half] = te
            bank_free[bank] += [te]

        def turn_p(g, t, half):
            bank = take_bank()
            ps = banks[bank][:].rearrange("p (h t) -> p h t", h=4)
            token = pe_job(bank, [transpose(ps[:, i], prob[:, t, 4 * half + i], ident32[:]) for i in range(4)],
                           after(("pexp", g, t, half)), sig["pturn"])
            done["pturn", g, t, half] = token
            hs = slice(4 * half, 4 * half + 4)
            split(bank, pt_hi[:, t, hs], pt_lo[:, t, hs], ps, 2.0 ** 13, [token, *after(("pv", g - 1, t))],
                  ("pt", g, t, half), sig["pt_hi"], sig["pt_lo"])

        def turn_sk(g, t):
            bank = take_bank()
            token = pe_job(bank, [transpose(banks[bank][:, c * P:(c + 1) * P], sk_t[:, c, t * P:(t + 1) * P], ident32[:])
                                  for c in range(NPAIR)], after(("sk", g, 0), ("sk", g, 1)), sig["skturn"])
            done["skturn", g, t] = token
            done["skrow", g, t] = act.add(actv(sk[:, t], banks[bank][:], ACT.Copy),
                                          [token, *after(("upd", g - 1, t))], sig["sk"])
            bank_free[bank] = [done["skrow", g, t]]

        def reset_memory(live):
            for t in range(TG):
                m = mem[:, live * TG + t]
                token = pool.add(lambda e, m=m: e.memset(m, 0.0), after(("mem", live, t)), sig["gp_work"])
                dve.add(lambda e, m=m: e.memset(m[0:DK, :, DV:DV1], 1.0 / DK), [token], sig["mem"])
                done["mem", live, t] = dve.add(
                    lambda e, m=m: e.memset(m[DK:P, :, 2 * DV1 - 1:2 * DV1], 1.0 / DK), (), sig["mem"])

        def read_memory(g, t):
            _, _, live = group_place(g)
            for j in range(2):
                bank = take_bank()
                ps = banks[bank][:, 0:2 * 2 * DV1].rearrange("p (c n) -> p c n", c=2)
                token = pe_job(bank, [matmul(ps[:, c], sq_t[:, 2 * j + c, t * P:(t + 1) * P],
                                             mem[:, live * TG + t, 2 * j + c], True, True) for c in range(2)],
                               after(("sq", g, 0), ("sq", g, 1), ("mem", live, t)), sig["num"])
                heads = ps.rearrange("p c (e n) -> p (c e) n", e=2)
                hs = slice(4 * j, 4 * j + 4)
                td = dve.add(lambda e, o=inv_den[:, t, hs], i=heads[:, :, DV]: e.reciprocal(o, i),
                             [token], sig["den"])
                tm = dve.add(tt(att_mem[:, t, hs], heads[:, :, 0:DV],
                                inv_den[:, t, hs].unsqueeze(2).to_broadcast([P, 4, DV]), ALU.mult),
                             [td, *after(("aturn", g - 1, t))], sig["mix_dve"])
                bank_free[bank] = [tm]
            done["num", g, t] = token
            done["att_mem", g, t] = tm

        def invert_sums(g, t, level):
            if level == 0:
                done["invsum", g, t] = dve.add(lambda e: e.reciprocal(inv_sum[:, t], row_sum[:, t]),
                                               [done["pexp", g, t, 0], done["pexp", g, t, 1]], sig["den"])
            else:
                done["mix", g, t] = dve.add(ts(dot_scale[:, t], inv_sum[:, t], gcol(g, G_V11), None, ALU.mult),
                                            after(("invsum", g, t), ("scal", g)), sig["den"])

        def attend(g, t):
            bank = take_bank()
            ps = banks[bank][:].rearrange("p (h v) -> p h v", h=H)
            calls = []
            for h in range(H):
                cols = slice(h * DV, (h + 1) * DV)
                terms = ((pt_hi, v_hi), (pt_hi, v_lo), (pt_lo, v_hi))
                calls += [matmul(ps[:, h], a[:, t, h], b[:, t, cols], m == 0, m == 2)
                          for m, (a, b) in enumerate(terms)]
            token = pe_job(bank, calls, after(("pt", g, t, 0), ("pt", g, t, 1), ("v", g, t)), sig["pv"])
            done["pv", g, t] = token
            ti = done["mix", g, t]
            tm = dve.add(tt(att_dot[:, t], ps, dot_scale[:, t].unsqueeze(2).to_broadcast([P, H, DV]), ALU.mult),
                         [token, ti, *after(("mixed", g - 1, t))], sig["mix_dve"])
            bank_free[bank] = [tm]
            a = att_mem[:, t].rearrange("p h v -> p (h v)")
            b = att_dot[:, t].rearrange("p h v -> p (h v)")
            t1 = pool.add(tt(a, a, gate_in[:], ALU.mult), after(("att_mem", g, t), "gates"), sig["mix_pool"])
            t2 = pool.add(tt(b, b, gate_out[:], ALU.mult), [tm], sig["mix_pool"])
            done["mixed", g, t] = pool.add(tt(a, a, b, ALU.add), [t1, t2], sig["mix_pool"])

        def update_memory(g, t):
            _, _, live = group_place(g)
            for j in range(2):
                bank = take_bank()
                ps = banks[bank][:, 0:2 * 2 * DV1].rearrange("p (c n) -> p c n", c=2)
                vv = v1[:, t].rearrange("p (c e) n -> p c (e n)", e=2)
                token = pe_job(bank, [matmul(ps[:, c], sk[:, t, (2 * j + c) * P:(2 * j + c + 1) * P],
                                             vv[:, 2 * j + c], True, True) for c in range(2)],
                               after(("skrow", g, t), ("v1", g, t)), sig["upd"])
                for rs, cs in ((slice(0, DK), slice(0, DV1)), (slice(DK, P), slice(DV1, 2 * DV1))):
                    m = mem[rs, live * TG + t, 2 * j:2 * j + 2, cs]
                    tm = dve.add(tt(m, ps[rs, :, cs], m, ALU.add), [token, *after(("mem", live, t))], sig["mem"])
                bank_free[bank] = [tm]
            done["upd", g, t] = token
            done["mem", live, t] = tm

        def turn_att(g, t):
            bank = take_bank()
            ps = banks[bank][:].rearrange("p (k c) -> p k c", k=KT)
            a = att_mem[:, t].rearrange("p h v -> p (h v)")
            token = pe_job(bank, [transpose(ps[:, k], a[:, k * P:(k + 1) * P], ident32[:]) for k in range(KT)],
                           after(("mixed", g, t)), sig["aturn"])
            done["aturn", g, t] = token
            split(bank, at_hi[:, t], at_lo[:, t], ps, gcol(g, G_ASCALE), [token, *after(("outscal", g), ("wo", g - 1, t))],
                  ("at", g, t), sig["at_hi"], sig["at_lo"])

        def layer_stats(g, t, which, waits):
            r = rows[:, g % NX, t]
            ta = dve.add(lambda e: e.bn_stats(stats[:, which, t], r), waits, sig["stat"])
            ta = dve.add(lambda e: e.bn_aggr(mean_var[:, which, t], stats[:, which, t]), [ta], sig["stat"])
            tb = pool.add(lambda e: e.tensor_scalar(var_eps[:, which, t:t + 1], mean_var[:, which, t, 1:2],
                                                    EPS, None, ALU.add), [ta], sig["pow_in"])
            done["rstd", g, t, which] = pool.add(
                tt(rstd[:, which, t:t + 1], var_eps[:, which, t:t + 1], minus_half[:], ALU.pow),
                [tb, t_half], sig["rstd"])

        def normalise(g, t, which):
            r = rows[:, g % NX, t]
            done["norm", g, t, which] = dve.add(
                ts(r, r, mean_var[:, which, t, 0:1], rstd[:, which, t:t + 1], ALU.subtract, ALU.mult),
                after(("rstd", g, t, which)), sig["norm"])

        def project_out(g, t):
            bank = take_bank()
            terms = [(xs[:, t, k], wt["o"][:, k, :]) for k in range(KT)
                     for xs, wt in ((at_hi, w_hi), (at_hi, w_lo), (at_lo, w_hi))]
            token = pe_job(bank, [matmul(banks[bank][:], a, b, i == 0, i == len(terms) - 1)
                                  for i, (a, b) in enumerate(terms)],
                           [done["at", g, t], done["wsplit", "o", 0], done["wsplit", "o", 1]], sig["wo"])
            done["wo", g, t] = token
            r = rows[:, g % NX, t]
            tr = dve.add(stt(r, banks[bank][:], gcol(g, G_WO), r, ALU.mult, ALU.add), [token], sig["resid"])
            bank_free[bank] = [tr]
            layer_stats(g, t, 0, [tr])

        def turn_y(g, t):
            bank = take_bank()
            ps = banks[bank][:].rearrange("p (k c) -> p k c", k=KT)
            r = rows[:, g % NX, t]
            token = pe_job(bank, [transpose(ps[:, k], r[:, k * P:(k + 1) * P], ident32[:]) for k in range(KT)],
                           after(("norm", g, t, 0)), sig["yturn"])
            toks = slice(t * P, (t + 1) * P)
            split(bank, yt_hi[:, g % 2, :, toks], yt_lo[:, g % 2, :, toks], ps, 2.0 ** 9,
                  [token, *after(("ffn1", g - 2, 7)), *([done["wturn", 31]] if g == 1 else [])], ("yt", g, t), sig["yt_hi"], sig["yt_lo"])
            done["yb", g, t] = pool.add(tt(r, r, b2_all[:], ALU.add), [token, t_small], sig["yb"])

        def ffn_up(g, j):
            bank = take_bank()
            ps = banks[bank][:].rearrange("p (c t) -> p c t", c=2)
            calls = []
            for c in range(2):
                cols = slice((2 * j + c) * P, (2 * j + c + 1) * P)
                terms = [(w1t[:, k, cols], ys[:, g % 2, k, :]) for k in range(KT) for ys in (yt_hi, yt_lo)]
                calls += [matmul(ps[:, c], a, b, i == 0, i == len(terms) - 1) for i, (a, b) in enumerate(terms)]
            token = pe_job(bank, calls, after(("yt", g, 0), ("yt", g, 1), ("wput", 1)), sig["ffn1"])
            done["ffn1", g, j] = token
            n = g * 8 + j
            buf = n % NH32
            for c in range(2):
                f = 2 * j + c
                tr = act.add(actv(h32[:, buf, c * GT:(c + 1) * GT], ps[:, c], ACT.Relu, scale=w(H_SCALE_Y),
                                  bias=b1_scaled[:, f:f + 1]),
                             [token, *after("hscale", ("h_lo", n - NH32), ("above", 2, 3, 3), ("below", 2, 3, 3))], sig["relu"])
            bank_free[bank] = [tr]
            hi = h_hi[:, 2 * j:2 * j + 2].rearrange("p f t -> p (f t)")
            lo = h_lo[:, 2 * j:2 * j + 2].rearrange("p f t -> p (f t)")
            th = dve.add(lambda e: e.tensor_copy(hi, h32[:, buf]), [tr, *after(("ffn2", g - 1, 1))], sig["h_hi"])
            q, s = (pool, sig["h_lo_pool"]) if j % 2 else (dve, sig["h_lo"])
            done["h_lo", n] = done["h", g, j] = q.add(tt(lo, h32[:, buf], hi, ALU.subtract),
                                                      [th, *after(("ffn2", g - 1, 1))], s)

        PIECES = 4

        def ffn_down(g, t, piece):
            own = RING + t
            toks = slice(t * P, (t + 1) * P)
            fs = range(piece * FT // PIECES, (piece + 1) * FT // PIECES)
            terms = [(hs[:, f, toks], w2t[:, f, :], f, hs is h_lo) for f in fs for hs in (h_hi, h_lo)]
            calls = [matmul(banks[own][:], a, b, f == 0 and not is_lo, f == FT - 1 and is_lo)
                     for a, b, f, is_lo in terms]
            last = piece == PIECES - 1
            waits = after(*[("h", g, f // 2) for f in fs], ("wput", 2)) + (bank_free[own] if piece == 0 else [])
            for i, call in enumerate(calls):
                token = pe.add(call, waits if i == 0 else (), sig["ffn2"] if last and i == len(calls) - 1 else None)
            if not last:
                return
            done["ffn2", g, t] = token
            r = rows[:, g % NX, t]
            tr = dve.add(stt(r, banks[own][:], w(H_INV), r, ALU.mult, ALU.add),
                         [token, *after(("yb", g, t), "hscale")], sig["resid"])
            bank_free[own] = [tr]
            layer_stats(g, t, 1, [tr])

        def put_out(g, t):
            b0, seg, _ = group_place(g)
            done["out", g, t] = sp.add(
                lambda e: e.dma_start(out[b0 + t, seg * P:(seg + 1) * P, :], rows[:, g % NX, t]),
                after(("norm", g, t, 1)), s_xout[g % NX][t], 16)

        QK, V, SC, T4 = 24 * 109, 12 * 216, 8 * 56, 4 * 109
        MEM, PV = 4 * 222, 24 * 34

        def turn_table(g):
            now, before, ahead = g < NG, 1 <= g <= NG, g + 1 < NG
            table = {}

            def step(name, when, cost, f, *args):
                table[name] = (when, cost, lambda: f(*args))

            for n in "kq":
                for j in range(2):
                    step(f"{n}{j}", now, QK, project_qk, g, n, j)
            for t in range(TG):
                step(f"v{t}", now, V, project_v, g, t)
                for half in range(2):
                    step(f"score{t}{half}", now, SC, scores, g, t, half)
                    step(f"turn_p{t}{half}", now, T4, turn_p, g, t, half)
                step(f"turn_sk{t}", now, T4, turn_sk, g, t)
                for level in range(2):
                    step(f"sums{t}{level}", now, 0, invert_sums, g, t, level)
                step(f"read{t}", now, MEM, read_memory, g, t)
                step(f"turn_x{t}", ahead, T4, turn_x, g + 1, t)
            for t, last, when in ((0, g, now), (1, g - 1, before)):
                step(f"attend{t}", when, PV, attend, last, t)
                step(f"update{t}", when, MEM, update_memory, last, t)
                step(f"turn_att{t}", when, T4, turn_att, last, t)
                step(f"out{t}", when, V, project_out, last, t)
                step(f"norm{t}", when, 0, normalise, last, t, 0)
                step(f"turn_y{t}", before, T4, turn_y, g - 1, t)
            step("max", ahead, 0, group_max, g + 1)
            for level in range(4):
                step(f"xscale{level}", ahead, 0, group_x_scale, g + 1, level)
            for level in range(3):
                step(f"scalars{level}", ahead, 0, group_scalars, g + 1, level)
            step("norm_end", g >= 2, 0, normalise, g - 2, 1, 1)
            step("put_end", g >= 2, 0, put_out, g - 2, 1)
            step("load", 1 <= g and g + 2 < NG, 0, load_x, g + 2)
            return table

        def attention_steps(g):
            table = turn_table(g)
            names = [half.split() for half in TURN]
            assert sorted(names[0] + names[1]) == sorted(table)
            return [[table[n][1:] for n in half if table[n][0]] for half in names]

        def ffn_steps(g):
            if not 0 <= g < NG:
                return [], []
            steps = [(16 * 109, lambda j=j: ffn_up(g, j)) for j in range(FT // 2)]
            for t in range(TG):
                for piece in range(PIECES):
                    steps.append((8 * 216, lambda t=t, p=piece: ffn_down(g, t, p)))
                    if t == 1 and piece == 0:
                        steps.append((0, lambda: normalise(g, 0, 1)))
                        steps.append((0, lambda: put_out(g, 0)))
            return steps[:EARLY], steps[EARLY:]

        def merged(a, b):
            total_a, total_b = sum(c for c, _ in a) or 1, sum(c for c, _ in b) or 1
            at_a = at_b = 0
            a, b = list(a), list(b)
            while a or b:
                if not b or (a and at_a / total_a <= at_b / total_b):
                    cost, f = a.pop(0)
                    at_a += cost
                else:
                    cost, f = b.pop(0)
                    at_b += cost
                f()

        def weight_block(n):
            def place(n):
                return 1 + n // 16, n // 4 % 4, n % 4

            if n < NBLOCKS:
                m, i, b = place(n)
                compare(m, i, b)
                if m == 1 and i >= 2 and b == 3:
                    load_ffn_w(2, i)
            if n:
                turn_w(*place(n - 1))

        load_x(1)
        load_x(2)
        for live in range(LIVE):
            reset_memory(live)
        table = {name: f for name, (when, _, f) in turn_table(0).items() if when}

        def start_step(name, f, *args):
            table[name] = lambda: f(*args)

        start_step("first_max", group_max, 0)
        for level in range(4):
            start_step(f"first_xscale{level}", group_x_scale, 0, level)
        for level in range(3):
            start_step(f"first_scalars{level}", group_scalars, 0, level)
        for t in range(TG):
            start_step(f"first_turn_x{t}", turn_x, 0, t)
        for n in "kqvo":
            start_step(f"max_{n}", max_w, n)
            start_step(f"scale_{n}", scale_w, n)
            for j in range(2):
                start_step(f"split_{n}{j}", split_w, n, j)
        start_step("gates", prepare_gates)
        start_step("ffn_scale", prepare_ffn_scale)
        for m in (1, 2):
            start_step(f"threshold{m}", threshold, m)
            for i in range(4):
                start_step(f"sum{m}{i}", sum_ffn_w, m, i)
        for m, i in ((1, 2), (1, 3), (2, 0), (2, 1)):
            start_step(f"load{m}{i}", load_ffn_w, m, i)
        order = START.split()
        assert sorted(n for n in order if n != "block") == sorted(table)
        made = 0
        for name in order:
            if name == "block":
                weight_block(made)
                made += 1
            else:
                table[name]()
        blocks = [(500, lambda n=n: weight_block(n)) for n in range(made, NBLOCKS + 1)]

        for g in range(1, NG + 2):
            if g < NG and g % (LIVE * NSEG) < LIVE and g >= LIVE * NSEG:
                reset_memory(group_place(g)[2])
            first, second = attention_steps(g)
            merged(first, ffn_steps(g - 2)[1] if g > 1 else blocks)
            merged(second, ffn_steps(g - 1)[0])

        sp.add(None, [(s.sem, s.count) for pair in s_xout for s in pair])

        block = ctx.enter_context(nc.Block())

        @block.sync
        def _(eng):
            sp.replay(eng)

        @block.tensor
        def _(eng):
            pe.replay(eng)

        @block.vector
        def _(eng):
            dve.replay(eng)

        @block.scalar
        def _(eng):
            act.replay(eng)

        @block.gpsimd
        def _(eng):
            pool.replay(eng)


_INS = ["L0_attn_x", "L0_attn_Wq", "L0_attn_Wk", "L0_attn_Wv", "L0_attn_betas", "L0_attn_Wo",
        "L0_ffn_W1", "L0_ffn_b1", "L0_ffn_W2", "L0_ffn_b2"]


def kernel(**inputs):
    import numpy as np
    import concourse.bacc as bacc
    from concourse.bass_utils import run_bass_kernel_spmd

    nc = bacc.Bacc("TRN2", target_bir_lowering=False, num_devices=1)
    arrays, args = {}, []
    for name in _INS:
        a = np.ascontiguousarray(inputs[name])
        arrays[f"in_{name}"] = a
        args.append(nc.dram_tensor(f"in_{name}", a.shape, mybir.dt.from_np(a.dtype), kind="ExternalInput").ap())
    shape = inputs["L0_attn_x"].shape
    args.append(nc.dram_tensor("out_rows", shape, F32, kind="ExternalOutput").ap())
    build_program(nc, *args)
    result = run_bass_kernel_spmd(nc, [arrays], core_ids=[0])
    return result.results[0]["out_rows"]
```
